# Optimizing a Trainium2 kernel written in Bass

```python
import numpy as np
import jax
import jax.numpy as jnp

def _softmax(x, axis=-1):
    return jax.nn.softmax(x, axis=axis)

def _gelu(x):
    return jax.nn.gelu(x, approximate=True)

def _silu(x):
    return jax.nn.silu(x)

def _sigmoid(x):
    return jax.nn.sigmoid(x)

def _layernorm(x, axis=-1, eps=1e-05):
    m = jnp.mean(x, axis=axis, keepdims=True)
    v = jnp.var(x, axis=axis, keepdims=True)
    return (x - m) / jnp.sqrt(v + eps)

def _scatter_add(tgt, idx, src, axis=0):
    return tgt.at[idx].add(src)

def _segment_sum(src, seg, n):
    return jax.ops.segment_sum(src, seg, n)
kernel_name = 'mk_decoder_preln_d1_seqx_r4_139960'

def setup_inputs(seed: int=0):
    np.random.seed(seed)
    _w = jnp.asarray

    def _rec_inputs():
        import jax
        import jax.numpy as jnp
        _rk = jax.random.key(seed)
        x = -0.0003929 + 0.9999 * jax.random.normal(jax.random.fold_in(_rk, 1), (8, 112, 512), jnp.float32)
        _lenS = 112 - jax.random.randint(jax.random.fold_in(_rk, 7), (8,), 0, max(1, 112 // 4) + 1, jnp.int32)
        _lenS2 = 375 - jax.random.randint(jax.random.fold_in(_rk, 8), (8,), 0, max(1, 375 // 4) + 1, jnp.int32)
        _ctx_2048P = jax.random.normal(jax.random.fold_in(_rk, 11), (8, 16, 512), jnp.float32)
        _ctx_2048c = jax.random.dirichlet(jax.random.fold_in(_rk, 511), 0.3 * jnp.ones((16,), jnp.float32), (8, 375))
        _ctx_2048t = jnp.einsum('bsk,bkd->bsd', _ctx_2048c, _ctx_2048P)
        _ctx_2048t = _ctx_2048t * jax.lax.rsqrt(jnp.mean(jnp.square(_ctx_2048t)) + 1e-12) * 0.953939
        ctx_2048 = -0.000514642 + 1.00011 * (_ctx_2048t + 0.3 * jax.random.normal(jax.random.fold_in(_rk, 611), (8, 375, 512), jnp.float32))
        return (x, ctx_2048)
    x, ctx_2048 = _rec_inputs()

    def _L0_attn_setup():
        import jax, jax.numpy as jnp
        import numpy as np
        key = jax.random.key(seed)
        ks = jax.random.split(key, 5)
        B, S, D = (1, 1024, 512)
        H, Dh = (16, 128)
        scale = 1.0 / np.sqrt(D).astype(np.float32)
        return {'x': jax.random.normal(ks[0], (B, S, D), dtype=jnp.float32), 'W_K': jax.random.normal(ks[1], (H, Dh, D), dtype=jnp.float32) * scale, 'W_Q': jax.random.normal(ks[2], (H, Dh, D), dtype=jnp.float32) * scale, 'W_V': jax.random.normal(ks[3], (H, Dh, D), dtype=jnp.float32) * scale, 'W_O': jax.random.normal(ks[4], (D, H * Dh), dtype=jnp.float32) * scale}
    _L0_attn_all = _L0_attn_setup()
    _L0_attn_in = {k: v for k, v in _L0_attn_all.items() if k in ('W_K', 'W_Q', 'W_V', 'W_O')}
    del _L0_attn_all

    def _L0_xattn_setup():
        import jax, jax.numpy as jnp
        import numpy as np
        DIM = 512
        NHEADS = 32
        HEAD_DIM = DIM // NHEADS
        EPS = 1e-06

        def _rmsnorm(t):
            return t * jax.lax.rsqrt(jnp.mean(t * t, axis=-1, keepdims=True) + EPS)
        key = jax.random.key(seed)
        kx, kc, kq, kk, kv = jax.random.split(key, 5)
        x = jax.random.normal(kx, (2, 1024, DIM), dtype=jnp.float32)
        context = jax.random.normal(kc, (2, 128, DIM), dtype=jnp.float32)
        std = 0.02
        Wq = jax.random.normal(kq, (DIM, DIM), dtype=jnp.float32) * std
        Wk = jax.random.normal(kk, (DIM, DIM), dtype=jnp.float32) * std
        Wv = jax.random.normal(kv, (DIM, DIM), dtype=jnp.float32) * std
        return {'x': x, 'context': context, 'Wq': Wq, 'Wk': Wk, 'Wv': Wv}
    _L0_xattn_all = _L0_xattn_setup()
    _L0_xattn_in = {k: v for k, v in _L0_xattn_all.items() if k in ('Wq', 'Wk', 'Wv')}
    del _L0_xattn_all

    def _L0_ffn_setup():
        import jax, jax.numpy as jnp
        import numpy as np
        H = 512
        I = 352
        E = 8
        TOP_K = 2
        N_SHARED = 2
        I_SH = I * N_SHARED
        NORM_TOPK = True

        def _moe_forward(hidden_states, gate_w, expert_gate, expert_up, expert_down, shared_gate, shared_up, shared_down):
            bsz, seq_len, hdim = hidden_states.shape
            x = hidden_states.reshape(-1, hdim)
            logits = x @ gate_w.T
            probs = jax.nn.softmax(logits, axis=-1)
            routing_weights, selected = jax.lax.top_k(probs, TOP_K)
            if NORM_TOPK:
                routing_weights = routing_weights / (routing_weights.sum(axis=-1, keepdims=True) + 1e-20)
            combine = jnp.sum(jax.nn.one_hot(selected, E, dtype=routing_weights.dtype) * routing_weights[..., None], axis=1)
            g_sh = x @ shared_gate.T
            u_sh = x @ shared_up.T
            out = jax.nn.silu(g_sh) * u_sh @ shared_down.T
            g = jnp.einsum('nh,eih->nei', x, expert_gate)
            u = jnp.einsum('nh,eih->nei', x, expert_up)
            y = jnp.einsum('nei,ehi->neh', jax.nn.silu(g) * u, expert_down)
            out = out + jnp.einsum('neh,ne->nh', y, combine)
            return out.reshape(bsz, seq_len, hdim)
        key = jax.random.key(seed)
        ks = jax.random.split(key, 8)
        s = 0.02
        return {'hidden_states': jax.random.normal(ks[0], (1, 256, H), dtype=jnp.float32), 'gate_w': jax.random.normal(ks[1], (E, H), dtype=jnp.float32) * s, 'expert_gate': jax.random.normal(ks[2], (E, I, H), dtype=jnp.float32) * s, 'expert_up': jax.random.normal(ks[3], (E, I, H), dtype=jnp.float32) * s, 'expert_down': jax.random.normal(ks[4], (E, H, I), dtype=jnp.float32) * s, 'shared_gate': jax.random.normal(ks[5], (I_SH, H), dtype=jnp.float32) * s, 'shared_up': jax.random.normal(ks[6], (I_SH, H), dtype=jnp.float32) * s, 'shared_down': jax.random.normal(ks[7], (H, I_SH), dtype=jnp.float32) * s}
    _L0_ffn_all = _L0_ffn_setup()
    _L0_ffn_in = {k: v for k, v in _L0_ffn_all.items() if k in ('gate_w', 'expert_gate', 'expert_up', 'expert_down', 'shared_gate', 'shared_up', 'shared_down')}
    del _L0_ffn_all
    return {'x': x, 'ctx_2048': ctx_2048, 'L0_attn_W_K': _L0_attn_in['W_K'], 'L0_attn_W_Q': _L0_attn_in['W_Q'], 'L0_attn_W_V': _L0_attn_in['W_V'], 'L0_attn_W_O': _L0_attn_in['W_O'], 'L0_xattn_Wq': _L0_xattn_in['Wq'], 'L0_xattn_Wk': _L0_xattn_in['Wk'], 'L0_xattn_Wv': _L0_xattn_in['Wv'], 'L0_ffn_gate_w': _L0_ffn_in['gate_w'], 'L0_ffn_expert_gate': _L0_ffn_in['expert_gate'], 'L0_ffn_expert_up': _L0_ffn_in['expert_up'], 'L0_ffn_expert_down': _L0_ffn_in['expert_down'], 'L0_ffn_shared_gate': _L0_ffn_in['shared_gate'], 'L0_ffn_shared_up': _L0_ffn_in['shared_up'], 'L0_ffn_shared_down': _L0_ffn_in['shared_down']}

def reference(x, ctx_2048, L0_attn_W_K, L0_attn_W_Q, L0_attn_W_V, L0_attn_W_O, L0_xattn_Wq, L0_xattn_Wk, L0_xattn_Wv, L0_ffn_gate_w, L0_ffn_expert_gate, L0_ffn_expert_up, L0_ffn_expert_down, L0_ffn_shared_gate, L0_ffn_shared_up, L0_ffn_shared_down):
    import jax
    import jax.numpy as jnp

    def _L0_attn_ref(x, W_K, W_Q, W_V, W_O):
        import jax, jax.numpy as jnp
        import numpy as np
        b, pos, d_model = x.shape
        d_head = W_K.shape[1]
        k = jnp.einsum('ihd,bpd->biph', W_K, x)
        q = jnp.einsum('ihd,bpd->biph', W_Q, x)
        v = jnp.einsum('ihd,bpd->biph', W_V, x)
        scores = jnp.einsum('biph,biqh->biqp', k, q)
        mask = jnp.tril(jnp.ones((pos, pos), dtype=x.dtype))
        masked = scores * mask - jnp.float32(10000000000.0) * (1.0 - mask)
        attn = jax.nn.softmax(masked / jnp.sqrt(jnp.float32(d_head)), axis=-1)
        z = jnp.einsum('biqp,biph->biqh', attn, v)
        z_flat = jnp.transpose(z, (0, 2, 1, 3)).reshape(b, pos, -1)
        out = jnp.einsum('df,bqf->bqd', W_O, z_flat)
        return out

    def _L0_xattn_ref(x, context, Wq, Wk, Wv):
        import jax, jax.numpy as jnp
        import numpy as np
        DIM = 512
        NHEADS = 32
        HEAD_DIM = DIM // NHEADS
        EPS = 1e-06

        def _rmsnorm(t):
            return t * jax.lax.rsqrt(jnp.mean(t * t, axis=-1, keepdims=True) + EPS)
        b, n, _ = x.shape
        m = context.shape[1]
        q = x @ Wq.T
        k_raw = context @ Wk.T
        v_raw = context @ Wv.T
        q = q.reshape(b, n, NHEADS, HEAD_DIM).transpose(0, 2, 1, 3)
        kv = jnp.concatenate([k_raw, v_raw], axis=-1)
        kv = kv.reshape(b, m, NHEADS, HEAD_DIM, 2)
        k = kv[..., 0].transpose(0, 2, 1, 3)
        v = kv[..., 1].transpose(0, 2, 1, 3)
        q = _rmsnorm(q)
        k = _rmsnorm(k)
        scale = HEAD_DIM ** (-0.5)
        scores = jnp.einsum('bhnd,bhmd->bhnm', q, k) * scale
        attn = jax.nn.softmax(scores, axis=-1)
        out = jnp.einsum('bhnm,bhmd->bhnd', attn, v)
        return out.transpose(0, 2, 1, 3).reshape(b, n, NHEADS * HEAD_DIM)

    def _L0_ffn_ref(hidden_states, gate_w, expert_gate, expert_up, expert_down, shared_gate, shared_up, shared_down):
        import jax, jax.numpy as jnp
        import numpy as np
        H = 512
        I = 352
        E = 8
        TOP_K = 2
        N_SHARED = 2
        I_SH = I * N_SHARED
        NORM_TOPK = True

        def _moe_forward(hidden_states, gate_w, expert_gate, expert_up, expert_down, shared_gate, shared_up, shared_down):
            bsz, seq_len, hdim = hidden_states.shape
            x = hidden_states.reshape(-1, hdim)
            logits = x @ gate_w.T
            probs = jax.nn.softmax(logits, axis=-1)
            routing_weights, selected = jax.lax.top_k(probs, TOP_K)
            if NORM_TOPK:
                routing_weights = routing_weights / (routing_weights.sum(axis=-1, keepdims=True) + 1e-20)
            combine = jnp.sum(jax.nn.one_hot(selected, E, dtype=routing_weights.dtype) * routing_weights[..., None], axis=1)
            g_sh = x @ shared_gate.T
            u_sh = x @ shared_up.T
            out = jax.nn.silu(g_sh) * u_sh @ shared_down.T
            g = jnp.einsum('nh,eih->nei', x, expert_gate)
            u = jnp.einsum('nh,eih->nei', x, expert_up)
            y = jnp.einsum('nei,ehi->neh', jax.nn.silu(g) * u, expert_down)
            out = out + jnp.einsum('neh,ne->nh', y, combine)
            return out.reshape(bsz, seq_len, hdim)
        return _moe_forward(hidden_states, gate_w, expert_gate, expert_up, expert_down, shared_gate, shared_up, shared_down)
    x = x + _L0_attn_ref(_layernorm(x, axis=-1), L0_attn_W_K, L0_attn_W_Q, L0_attn_W_V, L0_attn_W_O)
    x = x + _L0_xattn_ref(_layernorm(x, axis=-1), ctx_2048, L0_xattn_Wq, L0_xattn_Wk, L0_xattn_Wv)
    x = x + _L0_ffn_ref(_layernorm(x, axis=-1), L0_ffn_gate_w, L0_ffn_expert_gate, L0_ffn_expert_up, L0_ffn_expert_down, L0_ffn_shared_gate, L0_ffn_shared_up, L0_ffn_shared_down)
    return x

_drawn_inputs = setup_inputs


def setup_inputs(seed=0):
    import zlib

    import numpy as np

    out = dict(_drawn_inputs(seed))
    spreads = {}
    factors = {'L0_ffn_gate_w': 2.683}
    for name, (base, spread) in spreads.items():
        noise = np.random.default_rng([zlib.crc32(name.encode()), seed]).standard_normal(out[name].shape)
        drawn = base * np.exp(spread * noise) if base else spread * noise
        out[name] = jnp.asarray(drawn.astype(out[name].dtype))
    for name, factor in factors.items():
        out[name] = (out[name] * factor).astype(out[name].dtype)
    return out
```

```python
from contextlib import ExitStack

import concourse.bass as bass
from concourse import mybir

F32 = mybir.dt.float32
F32R = mybir.dt.float32r
U32 = mybir.dt.uint32
ALU = mybir.AluOpType
ACT = mybir.ActivationFunctionType
X = mybir.AxisListType.X

NB, T, D, NT = 8, 112, 512, 896
HT = NT // 2
KC = 4
NH, DH = 16, 128
M, MC, MS = 375, 3, 125
XH = 16
VW = 34
NE, NI, NCH = 8, 352, 28


class Queue:

    def __init__(self, name, sem):
        self.name, self.sem, self.n, self.ops, self.met = name, sem, 0, [], {}

    def needs(self, *tokens):
        for t in tokens:
            if t is None:
                continue
            if isinstance(t, list):
                self.needs(*t)
                continue
            key, sem, value = t
            if self.met.get(key, 0) < value:
                self.met[key] = value
                self.ops.append(("wait", sem, value))

    def __call__(self, fn, *tokens, inc=True):
        self.needs(*tokens)
        if inc:
            self.n += 1
            self.ops.append(("do", fn, self.sem))
            return (self.name, self.sem, self.n)
        self.ops.append(("do", fn, None))
        return None

    def load(self, fn, lane, *tokens):
        self.needs(*tokens)
        lane[2] += 16
        self.ops.append(("dma", fn, lane[1]))
        return (lane[0], lane[1], lane[2])

    def last(self):
        return (self.name, self.sem, self.n) if self.n else None

    def play(self, eng):
        for kind, a, b in self.ops:
            if kind == "wait":
                eng.wait_ge(a, b)
            elif kind == "dma":
                a(eng).then_inc(b, 16)
            elif b is None:
                a(eng)
            else:
                a(eng).then_inc(b, 1)


def decoder_layer(nc, x_d, ctx_d, wqk_d, wv_d, wo_d, wqx_d, wkv_d, gw_d, moe_d, ident_d, mask_d, iota_d, out_d):
    stack = ExitStack()
    with stack:
        place = [nc.sbuf_base + 63 & ~63]
        top = nc.sbuf_usable_end

        def sb(name, shape, dt):
            n = 4
            for s in shape[1:]:
                n *= s
            t = nc.alloc_sbuf_tensor_at(name, shape, dt, offset=place[0])
            place[0] += n + 31 & ~31
            assert place[0] <= top, (name, place[0], top)
            return t

        banks = [stack.enter_context(nc.psum_tensor(f"bank{i}", [128, 512], F32)) for i in range(8)]

        def queue(name):
            return Queue(name, stack.enter_context(nc.semaphore("q_" + name)))

        pe, act, dve, pool, sp = (queue(n) for n in ("pe", "act", "dve", "pool", "sp"))

        def lane(name):
            return [name, stack.enter_context(nc.semaphore("d_" + name)), 0]

        def mm(out, w, m, start, stop, *needs, inc=False):
            return pe(lambda e: e.matmul(out, w, m, start=start, stop=stop), *needs, inc=inc)

        def mm3(out, w, m, first, last, *needs, inc=False):
            mm(out, w[0], m[0], first, False, *needs)
            mm(out, w[1], m[0], False, False)
            return mm(out, w[0], m[1], False, last, inc=inc)

        def tr(out, in_, idn, *needs, inc=False):
            return pe(lambda e: e.transpose(out, in_, idn), *needs, inc=inc)

        def copy_act(out, in_, *needs):
            return act(lambda e: e.activation(out, in_, ACT.Copy), *needs)

        def copy_dve(out, in_, *needs):
            return dve(lambda e: e.tensor_copy(out, in_), *needs)

        def tt(q, out, a, b, op, *needs):
            return q(lambda e: e.tensor_tensor(out, a, b, op), *needs)

        def split(out, src, *needs, lo=None):
            th = copy_act(out[0], src, *needs)
            return tt(lo or dve, out[1], src, out[0].bitcast(F32), ALU.subtract, th)

        def pair(name, shape):
            return sb(name + "_hi", shape, F32R), sb(name + "_lo", shape, F32R)

        def at(p, *idx):
            return p[0].__getitem__(idx), p[1].__getitem__(idx)

        ident = sb("ident", [128, 128], F32)
        mask = sb("mask", [T, T], F32)
        xs = sb("xs", [T, NB, D], F32)
        xT = pair("xT", [128, KC, NT])
        st = sb("st", [T, NB, 6], F32)
        mv = sb("mv", [T, NB, 2], F32)
        ve = sb("ve", [T, NB], F32)
        rstd = sb("rstd", [T, NB], F32)
        half = sb("half", [128, 16], F32)
        xn = [sb(f"xn{i}", [T, D], F32) for i in range(2)]
        base = place[0]

        t_half = pool(lambda e: e.memset(half[:, :], -0.5))
        l_x = [lane("x0"), lane("x1")]
        l_c = lane("const")
        t_x = []
        for i in range(2):
            t_x.append(sp.load(lambda e, i=i: e.dma_start(
                xs[:, 4 * i:4 * i + 4, :], x_d[4 * i:4 * i + 4].rearrange("b t d -> t b d")), l_x[i]))
        t_id = sp.load(lambda e: e.dma_start(ident[:, :], ident_d), l_c)
        t_id = sp.load(lambda e: e.dma_start(mask[:, :], mask_d), l_c)

        xn_free = [None, None]
        n_xn = [0]

        def ln_stats(bs, *needs):
            a, z = bs[0], bs[-1] + 1
            for b in bs:
                t = dve(lambda e, b=b: e.bn_stats(st[:, b, :], xs[:, b, :]), *needs)
                t = dve(lambda e, b=b: e.bn_aggr(mv[:, b, :], st[:, b, :]), t)
            t = dve(lambda e: e.tensor_scalar(ve[:, a:z], mv[:, a:z, 1], 1e-5, None, ALU.add), t)
            return tt(pool, rstd[:, a:z], ve[:, a:z], half[0:T, 0:z - a], ALU.pow, t, t_half)

        def ln_apply(b, t_rstd, bank, free, x_free):
            i = n_xn[0] % 2
            n_xn[0] += 1
            t = dve(lambda e: e.tensor_scalar(xn[i][:, :], xs[:, b, :], mv[:, b, 0:1], rstd[:, b:b + 1],
                                              ALU.subtract, ALU.mult), t_rstd, xn_free[i])
            for k in range(KC):
                tp = tr(bank[:, k * T:(k + 1) * T], xn[i][:, k * 128:(k + 1) * 128], ident[0:T, 0:T],
                        t, t_id, free, inc=k == KC - 1)
            xn_free[i] = tp
            return split(at(xT, slice(None), slice(None), slice(b * T, (b + 1) * T)),
                         bank[:, 0:KC * T].rearrange("p (k t) -> p k t", k=KC), tp, x_free)

        wqk_f = [sb(f"wqk_f{i}", [128, KC, 256], F32) for i in range(2)]
        wqk = [pair(f"wqk{i}", [128, KC, 256]) for i in range(2)]
        wv_f = sb("wv_f", [128, KC, 256], F32)
        wv = pair("wv", [128, KC, 256])
        wo_f = sb("wo_f", [128, 2, D], F32)
        wo = pair("wo", [128, 2, D])
        qk = [pair(f"qk{i}", [128, 2, NT]) for i in range(2)]
        vv = pair("vv", [T, NB, 256])
        sm = [sb(f"sm{i}", [T, 4, T], F32) for i in range(2)]
        pp = [sb(f"pp{i}", [T, 4, T], F32) for i in range(2)]
        pt = [pair(f"pt{i}", [T, 4 * T]) for i in range(2)]
        zT = pair("zT", [128, 2, NT])
        nm = [sb(f"nm{i}", [T, 4], F32) for i in range(2)]
        rs = [sb(f"rs{i}", [T, 4], F32) for i in range(2)]
        rc = [sb(f"rc{i}", [T, 4], F32) for i in range(2)]
        l_wqk = [lane("wqk0"), lane("wqk1")]
        l_wv, l_wo = lane("wv"), lane("wo")
        wqk_stage = [None, None]
        wv_stage = wo_stage = None
        PJ, SB_, TB = banks[0:4], banks[4:6], banks[6:8]
        pj_free, s_free, tb_free = [None] * 4, [None] * 2, [None] * 2
        n_pj = [0]

        def pj_next():
            i = n_pj[0] % 4
            n_pj[0] += 1
            return i

        ISQ = 1.0 / float(DH) ** 0.5

        def prep_wqk(h, free):
            i = h % 2
            t = sp.load(lambda e: e.dma_start(wqk_f[i][:, :, :], wqk_d[h]), l_wqk[i], wqk_stage[i])
            t = split(at(wqk[i], slice(None)), wqk_f[i][:, :, :], t, free, lo=pool)
            wqk_stage[i] = t
            return t

        def prep_wv(p, free):
            nonlocal wv_stage
            t = sp.load(lambda e: e.dma_start(wv_f[:, :, :], wv_d[p]), l_wv, wv_stage)
            wv_stage = split(at(wv, slice(None)), wv_f[:, :, :], t, free, lo=pool)
            return wv_stage

        def prep_wo(p, free):
            nonlocal wo_stage
            t = sp.load(lambda e: e.dma_start(wo_f[:, :, :], wo_d[p]), l_wo, wo_stage)
            wo_stage = split(at(wo, slice(None)), wo_f[:, :, :], t, free, lo=pool)
            return wo_stage

        t_wqk = [None] * NH
        t_pj = [None] * NH
        t_qk = [None] * NH
        t_sc = [None] * NH
        t_wqk[0] = prep_wqk(0, None)
        t_wvp = prep_wv(0, None)
        t_wqk[1] = prep_wqk(1, None)
        t_wop = prep_wo(0, None)

        t_xT = [None] * NB
        for g in range(2):
            bs = list(range(4 * g, 4 * g + 4))
            t = ln_stats(bs, t_x[g])
            for b in bs:
                tb_free[b % 2] = t_xT[b] = ln_apply(b, t, TB[b % 2], tb_free[b % 2], None)

        def project_qk(h):
            w = wqk[h % 2]
            for n in range(2):
                for j in range(2):
                    i = pj_next()
                    for k in range(KC):
                        t = mm3(PJ[i][:, 0:HT], at(w, slice(None), k, slice(j * 128, j * 128 + 128)),
                                at(xT, slice(None), k, slice(n * HT, n * HT + HT)), k == 0, k == KC - 1,
                                t_wqk[h], t_xT[4 * n + 3], pj_free[i], inc=k == KC - 1)
                    pj_free[i] = split(at(qk[h % 2], slice(None), j, slice(n * HT, n * HT + HT)),
                                       PJ[i][:, 0:HT], t, t_sc[h - 2] if h >= 2 else None)
            t_pj[h] = t
            t_qk[h] = pj_free[i]

        t_av = [None] * NH
        t_v = None

        def project_v(p):
            nonlocal t_v
            for b in range(0, NB, 2):
                i = pj_next()
                for c in range(2):
                    for k in range(KC):
                        t = mm3(PJ[i][0:T, c * 256:c * 256 + 256],
                                at(xT, slice(None), k, slice((b + c) * T, (b + c + 1) * T)),
                                at(wv, slice(None), k, slice(None)), k == 0, k == KC - 1,
                                t_wvp, t_xT[b + c], pj_free[i], inc=k == KC - 1)
                pj_free[i] = split(at(vv, slice(None), slice(b, b + 2), slice(None)),
                                   PJ[i][0:T, :].rearrange("p (c n) -> p c n", c=2), t,
                                   t_av[2 * p - 1] if p else None)
            t_v = pj_free[i]
            return t

        t_sm = [None, None]
        t_pn = [None, None]
        t_pt_pe = [None, None]

        def scores(h):
            q = qk[h % 2]
            for g in range(2):
                for c in range(4):
                    b = 4 * g + c
                    t = mm3(SB_[g][0:T, c * T:(c + 1) * T], at(q, slice(None), 0, slice(b * T, (b + 1) * T)),
                            at(q, slice(None), 1, slice(b * T, (b + 1) * T)), True, True,
                            t_qk[h], s_free[g], inc=c == 3)
                t_sc[h] = t
                t = tt(dve, sm[g][:, :, :], SB_[g][0:T, 0:4 * T].rearrange("p (c t) -> p c t", c=4),
                       mask[:, :].unsqueeze(1).to_broadcast([T, 4, T]), ALU.add, t, t_id, t_sm[g])
                s_free[g] = t
                t = dve(lambda e, g=g: e.tensor_reduce(nm[g][:, :], sm[g][:, :, :], X, ALU.max, negate=True), t)
                t = dve(lambda e, g=g: e.tensor_scalar(nm[g][:, :], nm[g][:, :], ISQ, None, ALU.mult), t)
                for c in range(4):
                    t_sm[g] = act(lambda e, g=g, c=c: e.activation(
                        pp[g][:, c, :], sm[g][:, c, :], ACT.Exp, bias=nm[g][:, c:c + 1], scale=ISQ,
                        accum_out=rs[g][:, c:c + 1]), t, t_pt_pe[g])

        def normalise(h):
            for g in range(2):
                t = dve(lambda e, g=g: e.reciprocal(rc[g][:, :], rs[g][:, :]), t_sm[g])
                t_pn[g] = tt(dve, pp[g][:, :, :], pp[g][:, :, :],
                             rc[g][:, :].unsqueeze(2).to_broadcast([T, 4, T]), ALU.mult, t)

        t_pt = [None, None]

        def transpose_p(h):
            for g in range(2):
                for c in range(4):
                    t = tr(TB[g][0:T, c * T:(c + 1) * T], pp[g][:, c, :], ident[0:T, 0:T], t_pn[g], tb_free[g],
                           inc=c == 3)
                t_pt_pe[g] = t
                tb_free[g] = t_pt[g] = split(at(pt[g], slice(None), slice(None)), TB[g][0:T, 0:4 * T], t,
                                             t_av[h - 1] if h else None)

        t_wo_pe = None
        t_z = None

        def weighted_v(h):
            nonlocal t_z
            o = (h % 2) * 128
            for g in range(2):
                i = pj_next()
                for c in range(4):
                    b = 4 * g + c
                    t = mm3(PJ[i][:, c * T:(c + 1) * T], at(vv, slice(None), b, slice(o, o + 128)),
                            at(pt[g], slice(None), slice(c * T, (c + 1) * T)), True, True,
                            t_pt[g], t_v, pj_free[i], inc=c == 3)
                pj_free[i] = split(at(zT, slice(None), h % 2, slice(g * HT, g * HT + HT)), PJ[i][:, 0:HT], t, t_wo_pe)
            t_av[h] = t
            t_z = pj_free[i]

        t_res = [t_x[0]] * 4 + [t_x[1]] * 4

        def project_o(p):
            nonlocal t_wo_pe
            for b in range(NB):
                i = pj_next()
                for c in range(2):
                    t = mm3(PJ[i][0:T, :], at(zT, slice(None), c, slice(b * T, (b + 1) * T)),
                            at(wo, slice(None), c, slice(None)), c == 0, c == 1, t_z, t_wop, pj_free[i], inc=c == 1)
                pj_free[i] = t_res[b] = tt(dve, xs[:, b, :], xs[:, b, :], PJ[i][0:T, :], ALU.add, t, t_res[b])
            t_wo_pe = t

        project_qk(0)
        t_vpe = project_v(0)
        scores(0)
        normalise(0)
        for h in range(NH):
            if h + 1 < NH:
                project_qk(h + 1)
            if h + 2 < NH:
                t_wqk[h + 2] = prep_wqk(h + 2, t_pj[h])
            if h % 2 == 0 and h + 2 < NH:
                t_wvp = prep_wv(h // 2 + 1, t_vpe)
            transpose_p(h)
            if h + 1 < NH:
                scores(h + 1)
            weighted_v(h)
            if h + 1 < NH:
                normalise(h + 1)
            if h % 2:
                if h + 1 < NH:
                    t_vpe = project_v(h // 2 + 1)
                project_o(h // 2)
                if h + 1 < NH:
                    t_wop = prep_wo(h // 2 + 1, t_wo_pe)

        done_a = [q.last() for q in (pe, act, dve, pool)]

        end_a = place[0]
        place[0] = base
        NU = 2 * NB
        ctx_f = [sb(f"ctx_f{i}", [128, KC, MS], F32) for i in range(2)]
        ctx = [pair(f"ctx{i}", [128, KC, MS]) for i in range(4)]
        vb = [sb(f"vb{i}", [MS, MC, XH, VW], F32R) for i in range(2)]
        sq = [sb(f"sq{i}", [MS, 256], F32) for i in range(2)]
        kn = [sb(f"kn{i}", [MS, 256], F32) for i in range(2)]
        ss = [sb(f"ss{i}", [MS, XH], F32) for i in range(2)]
        rr = [sb(f"rr{i}", [MS, XH], F32) for i in range(2)]
        kk = [sb(f"kk{i}", [MS, XH, 4, 16], F32R) for i in range(2)]
        kT = [sb(f"kT{i}", [128, 8, M], F32R) for i in range(2)]
        wx_f = nc.alloc_sbuf_tensor_at("wx_f", [128, 1024], F32, offset=place[0] - 12000)
        qT = [sb(f"qT{i}", [128, 8, 2, T], F32R) for i in range(2)]
        ee = [sb(f"ee{i}", [MS, 4 * T], F32) for i in range(2)]
        ep = [pair(f"ep{i}", [MS, 4 * T]) for i in range(6)]
        oo = [sb(f"oo{i}", [VW, 4 * T], F32) for i in range(1)]
        zz = sb("zz", [T, 4, 16], F32)
        zc = sb("zc", [T, 4], F32)
        gw_f = sb("gw_f", [128, KC, NE], F32)
        gw = pair("gw", [128, KC, NE])
        pr = sb("pr", [T, NE], F32)
        r1 = sb("r1", [T, 4], F32)
        mx8 = sb("mx8", [T, 8], F32)
        ix8 = sb("ix8", [T, 8], U32)
        ixf = sb("ixf", [T, 8], F32)
        w2 = sb("w2", [T, 2], F32)
        cm0 = sb("cm0", [T, NE], F32)
        cm1 = sb("cm1", [T, NE], F32)
        comb = sb("comb", [T, NB, NE], F32)
        iot = sb("iot", [T, NE], F32)
        wqx = pair("wqx", [128, KC, D])
        wkv = pair("wkv", [128, KC, 2, D])
        end_b = place[0]

        l_wx, l_cx = lane("wx"), [lane("cx0"), lane("cx1")]
        t_wx = list(done_a)

        t = None
        t_wkv = []
        for k in range(KC):
            t = sp.load(lambda e, k=k: e.dma_start(wx_f[:, :], wkv_d[:, k * 1024:(k + 1) * 1024]), l_wx, done_a, t)
            t = split(at(wkv, slice(None), k), wx_f[:, :].rearrange("p (a n) -> p a n", a=2), t, done_a, lo=pool)
            t_wkv.append(t)
        t_wkv = t
        for k in range(2):
            t = sp.load(lambda e, k=k: e.dma_start(wx_f[:, :], wqx_d[:, k * 1024:(k + 1) * 1024]), l_wx, t)
            t = split(at(wqx, slice(None), slice(2 * k, 2 * k + 2)),
                      wx_f[:, :].rearrange("p (a n) -> p a n", a=2), t, done_a, lo=pool)
        t_wqx = t
        t = sp.load(lambda e: e.dma_start(gw_f[:, :, :], gw_d), l_wx, t)
        t_iot = sp.load(lambda e: e.dma_start(iot[:, :], iota_d), l_wx)
        t_gw = split(at(gw, slice(None)), gw_f[:, :, :], t_iot, done_a, lo=pool)
        t_one = None
        for i in range(2):
            t_one = pool(lambda e, i=i: e.memset(vb[i][:, :, :, 32:33].bitcast(F32), 1.0), done_a)
            t_one = pool(lambda e, i=i: e.memset(vb[i][:, :, :, 33:34].bitcast(F32), 0.0), done_a)
            t_one = pool(lambda e, i=i: e.memset(qT[i][:, :, :, :].bitcast(F32), 0.0), done_a)

        KB, SX, AB, TX = banks[0:2], banks[2:5], banks[5], banks[6:8]
        kb_free, sx_free, tx_free = [done_a] * 2, [done_a] * 3, [done_a] * 2
        ab_free = done_a
        n_kb, n_sx, n_tx, n_ep = [0], [0], [0], [0]

        def turn(c, n):
            i = c[0] % n
            c[0] += 1
            return i

        ctx_stage = [done_a, done_a]
        ctx_use = [done_a] * 4
        t_ctx = {}

        def load_ctx(b, m):
            n = b * MC + m
            i, j = n % 2, n % 4
            t = sp.load(lambda e: e.dma_start(ctx_f[i][:, :, :], ctx_d[b, m]), l_cx[i], ctx_stage[i])
            ctx_stage[i] = t_ctx[b, m] = split(at(ctx[j], slice(None)), ctx_f[i][:, :, :], t, ctx_use[j], lo=pool)

        vb_free, kT_free, qT_free = [done_a] * 2, [done_a, t_wqx], [done_a] * 2
        sq_free, kn_free, kk_free = [done_a] * 2, [done_a] * 2, [done_a] * 2
        t_kT, t_qT, t_vb = [None] * NU, [None] * NU, [None] * NU
        rows = {}
        n_row = [0]

        def rms(i, src, R, t):
            t = act(lambda e: e.activation(sq[i][0:R, :], src, ACT.Square), t, sq_free[i])
            t_sq = t
            t = dve(lambda e: e.tensor_reduce(ss[i][0:R, :], sq[i][0:R, :].rearrange("p (h d) -> p h d", d=16),
                                              X, ALU.add), t, kn_free[i])
            sq_free[i] = t
            t = dve(lambda e: e.tensor_scalar(ss[i][0:R, :], ss[i][0:R, :], 1.0 / 16, 1e-6, ALU.mult, ALU.add), t)
            return t_sq, tt(pool, rr[i][0:R, :], ss[i][0:R, :], half[0:R, 0:XH], ALU.pow, t, t_half)

        def kv_rows(u, m):
            b, hf = u // 2, u % 2
            j = (b * MC + m) % 4
            i = turn(n_kb, 2)
            for k in range(KC):
                t = mm3(KB[i][0:MS, :], at(ctx[j], slice(None), k, slice(None)),
                        at(wkv, slice(None), k, hf, slice(None)), k == 0, k == KC - 1,
                        t_ctx[b, m], t_wkv, kb_free[i], inc=k == KC - 1)
            ctx_use[j] = t
            r = turn(n_row, 2)
            src = KB[i][0:MS, 0:256]
            t_sq, t_r = rms(r, src, MS, t)
            v = KB[i][0:MS, 256:512].rearrange("p (h d) -> p h d", d=16)
            vh, vl = vb[u % 2][:, m, :, 0:16], vb[u % 2][:, m, :, 16:32]
            t = copy_act(vh, v, t, vb_free[u % 2], t_one)
            t_vb[u] = tt(dve, vl, v, vh.bitcast(F32), ALU.subtract, t, vb_free[u % 2])
            rows[u, m] = (i, r, src, MS, [t_sq, t_r, t_vb[u]])

        def q_rows(u):
            b, hf = u // 2, u % 2
            i = turn(n_kb, 2)
            for k in range(KC):
                t = mm3(KB[i][0:T, 0:256], at(xT, slice(None), k, slice(b * T, (b + 1) * T)),
                        at(wqx, slice(None), k, slice(hf * 256, hf * 256 + 256)), k == 0, k == KC - 1,
                        t_xT2[b], t_wqx, kb_free[i], inc=k == KC - 1)
            r = turn(n_row, 2)
            t_sq, t_r = rms(r, KB[i][0:T, 0:256], T, t)
            rows[u, "q"] = (i, r, KB[i][0:T, 0:256], T, [t_sq, t_r])

        def finish_rows(u, m):
            i, r, src, R, t = rows.pop((u, m))
            t = tt(dve, kn[r][0:R, :].rearrange("p (h d) -> p h d", d=16), src.rearrange("p (h d) -> p h d", d=16),
                   rr[r][0:R, :].unsqueeze(2).to_broadcast([R, XH, 16]), ALU.mult, t, kn_free[r])
            kb_free[i] = t
            row = kn[r][0:R, :].rearrange("p (h d) -> p h d", d=16)
            twice = row.unsqueeze(2).to_broadcast([R, XH, 2, 16])
            o = kk[r][0:R, :, :, :]
            if m == "q":
                hi, lo, first = o[:, :, 0:2, :], o[:, :, 2:4, :], o[:, :, 0, :]
            else:
                o = o.rearrange("p h (a c) d -> p h a c d", c=2)
                hi, lo, first = o[:, :, :, 0, :], o[:, :, :, 1, :], kk[r][0:R, :, 0, :]
            t = copy_dve(hi, twice, t, kk_free[r])
            first2 = first.bitcast(F32).unsqueeze(2).to_broadcast([R, XH, 2, 16])
            t = tt(dve, lo, twice, first2, ALU.subtract, t)
            kn_free[r] = t
            rows[u, m] = (r, R, t)

        def turn_rows(u, m):
            r, R, t = rows.pop((u, m))
            s = kk[r][0:R, :, :, :].bitcast(F32).rearrange("p (g h) a d -> p g (h a d)", h=2)
            for c in range(2):
                i = turn(n_tx, 2)
                for g in range(4):
                    tp = tr(TX[i][:, g * R:(g + 1) * R], s[:, 4 * c + g, :], ident[0:R, 0:R], t, tx_free[i], inc=g == 3)
                src = TX[i][:, 0:4 * R].rearrange("p (g t) -> p g t", g=4)
                if m == "q":
                    for o in range(2):
                        tx_free[i] = copy_act(qT[u % 2][64 * o:64 * o + 64, 4 * c:4 * c + 4, o, :],
                                              src[64 * o:64 * o + 64], tp, qT_free[u % 2], t_one)
                    t_qT[u] = tx_free[i]
                else:
                    tx_free[i] = copy_act(kT[u % 2][:, 4 * c:4 * c + 4, m * MS:(m + 1) * MS], src, tp, kT_free[u % 2])
                    t_kT[u] = tx_free[i]
            kk_free[r] = tp

        ee_free, ep_free = [done_a] * 2, [done_a] * 6
        oo_free = [done_a] * 2
        probs = {}
        outs = {}
        n_ee = [0]
        n_oo = [0]

        def score_quad(u, q):
            for m in range(MC):
                i = turn(n_sx, 3)
                for c in range(2):
                    t = mm(SX[i][0:MS, c * 2 * T:(c + 1) * 2 * T], kT[u % 2][:, 2 * q + c, m * MS:(m + 1) * MS],
                           qT[u % 2][:, 2 * q + c, :, :], True, True, t_kT[u], t_qT[u], sx_free[i], inc=c == 1)
                if m == MC - 1 and q == 3:
                    kT_free[u % 2] = qT_free[u % 2] = t
                e, p = turn(n_ee, 2), turn(n_ep, 6)
                t = act(lambda en, e=e, i=i: en.activation(ee[e][:, :], SX[i][0:MS, 0:4 * T], ACT.Exp, scale=0.25),
                        t, ee_free[e])
                sx_free[i] = t
                t = copy_dve(ep[p][0][:, :], ee[e][:, :], t, ep_free[p])
                t = tt(dve, ep[p][1][:, :], ee[e][:, :], ep[p][0][:, :].bitcast(F32), ALU.subtract, t)
                ee_free[e] = t
                probs[u, q, m] = (p, t)

        def value_quad(u, q):
            nonlocal ab_free
            for c in range(4):
                for m in range(MC):
                    p, t = probs[u, q, m]
                    w = vb[u % 2][:, m, 4 * q + c, :]
                    o = AB[0:VW, c * T:(c + 1) * T]
                    mm(o, w, ep[p][0][:, c * T:(c + 1) * T], m == 0, False, t, t_vb[u], t_one, ab_free)
                    t = mm(o, w, ep[p][1][:, c * T:(c + 1) * T], False, m == MC - 1, inc=c == 3)
                    if c == 3:
                        ep_free[p] = t
            if q == 3:
                vb_free[u % 2] = t
            i = turn(n_oo, 1)
            ab_free = copy_act(oo[i][:, :], AB[0:VW, 0:4 * T], t, oo_free[i])
            outs[u, q] = (i, ab_free)

        t_zz = done_a

        def out_quad(u, q):
            nonlocal t_zz
            b, hf = u // 2, u % 2
            i, t = outs.pop((u, q))
            j = turn(n_tx, 2)
            for c in range(4):
                tp = tr(TX[j][0:T, c * VW:(c + 1) * VW], oo[i][:, c * T:(c + 1) * T], ident[0:VW, 0:VW], t,
                        tx_free[j], inc=c == 3)
            oo_free[i] = tp
            o = TX[j][0:T, 0:4 * VW].rearrange("p (c w) -> p c w", w=VW)
            t0 = dve(lambda e: e.reciprocal(zc[:, :], o[:, :, 32]), tp, t_zz)
            t1 = dve(lambda e: e.tensor_reduce(zz[:, :, :], o[:, :, 0:32].rearrange("p c (a d) -> p c d a", a=2),
                                               X, ALU.add), tp, t_zz)
            tx_free[j] = t1
            t = tt(dve, zz[:, :, :], zz[:, :, :], zc[:, :].unsqueeze(2).to_broadcast([T, 4, 16]), ALU.mult, t0, t1)
            n = (hf * XH + 4 * q) * 16
            t_zz = t_res[b] = tt(dve, xs[:, b, n:n + 64].rearrange("p (c d) -> p c d", d=16),
                                 xs[:, b, n:n + 64].rearrange("p (c d) -> p c d", d=16), zz[:, :, :], ALU.add,
                                 t, t_res[b])

        t_xT3, t_comb = [None] * NB, [None] * NB
        t_q_pe = [None] * NB
        t_rt = done_a

        def route(b):
            nonlocal t_rt
            t = ln_stats([b], t_res[b])
            j = turn(n_tx, 2)
            tx_free[j] = t_xT3[b] = ln_apply(b, t, TX[j], tx_free[j], t_q_pe[b])
            i = turn(n_kb, 2)
            for k in range(KC):
                t = mm3(KB[i][0:T, 0:NE], at(xT, slice(None), k, slice(b * T, (b + 1) * T)),
                        at(gw, slice(None), k, slice(None)), k == 0, k == KC - 1, t_xT3[b], t_gw, kb_free[i],
                        inc=k == KC - 1)
            l = KB[i][0:T, 0:NE]
            t = dve(lambda e: e.tensor_reduce(r1[:, 0:1], l, X, ALU.max, negate=True), t, t_rt)
            t = act(lambda e: e.activation(pr[:, :], l, ACT.Exp, bias=r1[:, 0:1], accum_out=r1[:, 1:2]), t)
            kb_free[i] = t
            t = dve(lambda e: e.reciprocal(r1[:, 2:3], r1[:, 1:2]), t)
            t = dve(lambda e: e.tensor_scalar(pr[:, :], pr[:, :], r1[:, 2:3], None, ALU.mult), t)
            t = dve(lambda e: e.max(mx8[:, :], pr[:, :]), t)
            t0 = dve(lambda e: e.max_index(ix8[:, :], mx8[:, :], pr[:, :]), t)
            t0 = copy_dve(ixf[:, :], ix8[:, :], t0)
            t = tt(dve, r1[:, 3:4], mx8[:, 0:1], mx8[:, 1:2], ALU.add, t)
            t = dve(lambda e: e.tensor_scalar(r1[:, 3:4], r1[:, 3:4], 1e-20, None, ALU.add), t)
            t = dve(lambda e: e.reciprocal(r1[:, 3:4], r1[:, 3:4]), t)
            t = dve(lambda e: e.tensor_scalar(w2[:, :], mx8[:, 0:2], r1[:, 3:4], None, ALU.mult), t)
            ta = dve(lambda e: e.tensor_scalar(cm0[:, :], iot[:, :], ixf[:, 0:1], w2[:, 0:1], ALU.is_equal, ALU.mult),
                     t, t0, t_iot)
            tb = dve(lambda e: e.tensor_scalar(cm1[:, :], iot[:, :], ixf[:, 1:2], w2[:, 1:2], ALU.is_equal, ALU.mult),
                     t, t0)
            t_rt = t_comb[b] = tt(dve, comb[:, b, :], cm0[:, :], cm1[:, :], ALU.add, ta, tb)

        load_ctx(0, 0)
        load_ctx(0, 1)
        kv_rows(0, 0)
        finish_rows(0, 0)
        load_ctx(0, 2)
        t = ln_stats(list(range(NB)), t_res)
        t_xT2 = [None] * NB
        for b in range(NB):
            j = turn(n_tx, 2)
            tx_free[j] = t_xT2[b] = ln_apply(b, t, TX[j], tx_free[j], done_a)
        turn_rows(0, 0)
        kv_rows(0, 1)
        finish_rows(0, 1)
        turn_rows(0, 1)
        kv_rows(0, 2)
        finish_rows(0, 2)
        turn_rows(0, 2)
        q_rows(0)
        finish_rows(0, "q")
        turn_rows(0, "q")
        score_quad(0, 0)
        for u in range(NU):
            n = u + 1 if u + 1 < NU else None

            def ahead(f, *a):
                if n is not None:
                    f(n, *a)

            if n is not None and n % 2 == 1 and n // 2 + 1 < NB:
                load_ctx(n // 2 + 1, 0)
            score_quad(u, 1)
            ahead(kv_rows, 0)
            if n is not None and n % 2 == 1 and n // 2 + 1 < NB:
                load_ctx(n // 2 + 1, 1)
            value_quad(u, 0)
            ahead(finish_rows, 0)
            ahead(q_rows)
            if n is not None:
                t_q_pe[n // 2] = pe.last()
            score_quad(u, 2)
            out_quad(u, 0)
            ahead(turn_rows, 0)
            ahead(finish_rows, "q")
            ahead(kv_rows, 1)
            if n is not None and n % 2 == 1 and n // 2 + 1 < NB:
                load_ctx(n // 2 + 1, 2)
            value_quad(u, 1)
            ahead(turn_rows, "q")
            ahead(finish_rows, 1)
            score_quad(u, 3)
            out_quad(u, 1)
            ahead(kv_rows, 2)
            ahead(turn_rows, 1)
            value_quad(u, 2)
            ahead(finish_rows, 2)
            out_quad(u, 2)
            value_quad(u, 3)
            ahead(turn_rows, 2)
            if n is not None:
                score_quad(n, 0)
            out_quad(u, 3)
            if u % 2:
                route(u // 2)

        done_b = [q.last() for q in (pe, act, dve, pool)]

        place[0] = end_b
        bc = sb("bc", [128, NE, NT], F32) if False else None
        comb_end = end_b
        place[0] = base
        bc = sb("bc", [128, NE, NT], F32)
        we_f = [sb(f"we_f{i}", [128, 1536], F32) for i in range(2)]
        assert place[0] < (nc.sbuf_base + 63 & ~63) + 16384 * 16
        sg = [sb(f"sg{i}", [128, HT], F32) for i in range(2)]
        hh = [sb(f"hh{i}", [128, HT], F32) for i in range(2)]
        hs = [pair(f"hs{i}", [128, HT]) for i in range(2)]
        yo = [sb(f"yo{i}", [T, D], F32) for i in range(2)]
        cmc = sb("cmc", [T, NB, NE], F32)
        we = [pair(f"we{i}", [128, 1536]) for i in range(2)]

        AC, GU = banks[0:4], banks[4:8]
        ac_free, gu_free = [done_b] * 4, [done_b] * 4
        n_gu = [0]
        t_cmc = copy_dve(cmc[:, :, :], comb[:, :, :], done_b)
        for e_ in range(NE):
            for n in range(2):
                i = turn(n_gu, 4)
                for c in range(4):
                    b = 4 * n + c
                    t = mm(GU[i][:, c * T:(c + 1) * T], cmc[:, b, e_:e_ + 1].to_broadcast([T, 128]), ident[0:T, 0:T],
                           True, True, t_cmc, gu_free[i], inc=c == 3)
                gu_free[i] = t_bc = copy_act(bc[:, e_, n * HT:(n + 1) * HT], GU[i][:, 0:HT], t)

        l_we = [lane("we0"), lane("we1")]
        l_out = [lane("out0"), lane("out1")]
        we_stage = [done_b, done_b]
        we_free = [done_b, done_b]
        t_bcs = act.last()

        def load_chunk(s):
            c = s % NCH
            i = s % 2
            t = sp.load(lambda e: e.dma_start(we_f[i][:, :], moe_d[c]), l_we[i], we_stage[i])
            t = copy_act(we[i][0][:, :], we_f[i][:, :], t, we_free[i])
            we_stage[i] = tt(pool, we[i][1][:, :], we_f[i][:, :], we[i][0][:, :].bitcast(F32), ALU.subtract, t)
            return we_stage[i]

        sg_free, hh_free, hs_free = [done_b] * 2, [done_b] * 2, [done_b] * 2
        yo_free = [done_b] * 2
        t_we = {0: load_chunk(0), 1: load_chunk(1)}
        t_hs = {}

        def up(s):
            n, c, w = s // NCH, s % NCH, we[s % 2]
            i = [turn(n_gu, 4), turn(n_gu, 4)]
            tg = []
            for a in range(2):
                for k in range(KC):
                    o = k * 256 + a * 128
                    t = mm3(GU[i[a]][:, 0:HT], at(w, slice(None), slice(o, o + 128)),
                            at(xT, slice(None), k, slice(n * HT, n * HT + HT)), k == 0, k == KC - 1,
                            t_we[s], t_xT3, gu_free[i[a]], inc=k == KC - 1)
                tg.append(t)
            j = s % 2
            t = act(lambda e: e.activation(sg[j][:, :], GU[i[0]][:, 0:HT], ACT.Silu), tg[0], sg_free[j])
            gu_free[i[0]] = t
            t = tt(dve, hh[j][:, :], sg[j][:, :], GU[i[1]][:, 0:HT], ALU.mult, t, tg[1], hh_free[j])
            gu_free[i[1]] = sg_free[j] = t
            r = 0
            while r < 128 and c * 128 + r < NE * NI:
                x_ = (c * 128 + r) // NI
                z = min(128, (x_ + 1) * NI - c * 128)
                z = min(z, r + 32 if r in (32, 96) else r + 64 if r == 64 else 128)
                tm = tt(dve, hh[j][r:z, :], hh[j][r:z, :], bc[r:z, x_, n * HT:(n + 1) * HT], ALU.mult, t, t_bcs)
                r = z
            t = [t, dve.last()]
            hh_free[j] = t_hs[s] = split(at(hs[j], slice(None), slice(None)), hh[j][:, :], t, hs_free[j])

        t_end = []

        def down(s):
            n, c, w = s // NCH, s % NCH, we[s % 2]
            j = s % 2
            for b in range(4):
                t = mm3(AC[b][0:T, :], at(hs[j], slice(None), slice(b * T, (b + 1) * T)),
                        at(w, slice(None), slice(1024, 1536)), c == 0, c == NCH - 1, t_hs[s], ac_free[b], inc=True)
                if c == NCH - 1:
                    y = b % 2
                    bb = 4 * n + b
                    ac_free[b] = tt(dve, yo[y][:, :], xs[:, bb, :], AC[b][0:T, :], ALU.add, t, yo_free[y])
                    yo_free[y] = sp.load(lambda e, y=y, bb=bb: e.dma_start(out_d[bb], yo[y][:, :]), l_out[y], ac_free[b])
                    t_end.append(yo_free[y])
            hs_free[j] = t
            we_free[j] = t

        for s in range(2 * NCH + 1):
            if s < 2 * NCH:
                up(s)
            if s >= 1:
                down(s - 1)
                if s + 1 < 2 * NCH:
                    t_we[s + 1] = load_chunk(s + 1)
        sp.needs(*t_end)

        with nc.Block() as block:
            block.sync(sp.play)
            block.gpsimd(pool.play)
            block.scalar(act.play)
            block.vector(dve.play)
            block.tensor(pe.play)


def kernel(x, ctx_2048, L0_attn_W_K, L0_attn_W_Q, L0_attn_W_V, L0_attn_W_O, L0_xattn_Wq, L0_xattn_Wk, L0_xattn_Wv,
           L0_ffn_gate_w, L0_ffn_expert_gate, L0_ffn_expert_up, L0_ffn_expert_down, L0_ffn_shared_gate,
           L0_ffn_shared_up, L0_ffn_shared_down):
    import numpy as np
    import concourse.bacc as bacc
    from concourse.bass_utils import run_bass_kernel_spmd

    def c(a):
        return np.ascontiguousarray(a)

    def inner(a):
        a = np.asarray(a)
        a = np.swapaxes(a, -1, -2)
        a = a.reshape(a.shape[:-2] + (KC, 128, a.shape[-1]))
        return np.swapaxes(a, -2, -3)

    wk, wq, wv = (np.asarray(a) for a in (L0_attn_W_K, L0_attn_W_Q, L0_attn_W_V))
    wqk = inner(np.concatenate([wq, wk], axis=1))
    wvp = inner(wv.reshape(NH // 2, 2 * DH, D))
    wo = np.asarray(L0_attn_W_O).T.reshape(NH // 2, 2, DH, D).transpose(0, 2, 1, 3)
    ctx = inner(np.asarray(ctx_2048).reshape(NB, MC, MS, D))
    wcat = np.concatenate([np.asarray(L0_xattn_Wk), np.asarray(L0_xattn_Wv)], axis=0)
    wcat = wcat.reshape(2, XH, 16, 2, D).transpose(0, 3, 1, 2, 4).reshape(2 * 512, D)
    wkv = inner(wcat).reshape(128, KC * 1024)
    wqx = inner(L0_xattn_Wq).reshape(128, KC * D)
    gw = inner(L0_ffn_gate_w)
    up = np.zeros((2, NCH * 128, D), np.float32)
    n = NE * NI
    for i, (a, b) in enumerate(((L0_ffn_expert_gate, L0_ffn_shared_gate), (L0_ffn_expert_up, L0_ffn_shared_up))):
        up[i, :n] = np.asarray(a).reshape(n, D)
        up[i, n:n + 2 * NI] = np.asarray(b)
    dn = np.zeros((NCH * 128, D), np.float32)
    dn[:n] = np.asarray(L0_ffn_expert_down).transpose(0, 2, 1).reshape(n, D)
    dn[n:n + 2 * NI] = np.asarray(L0_ffn_shared_down).T
    upc = inner(up.reshape(2, NCH, 128, D).transpose(1, 0, 2, 3).reshape(NCH, 256, D)).reshape(NCH, 128, KC * 256)
    moe = np.concatenate([upc, dn.reshape(NCH, 128, D)], axis=2)
    i = np.arange(T)
    arrays = {
        "x": c(x), "ctx": c(ctx), "wqk": c(wqk), "wv": c(wvp), "wo": c(wo), "wqx": c(wqx), "wkv": c(wkv), "gw": c(gw),
        "moe": c(moe), "ident": np.eye(128, dtype=np.float32),
        "mask": np.where(i[:, None] >= i[None, :], 0.0, -1e10).astype(np.float32),
        "iota": np.tile(np.arange(NE, dtype=np.float32), (T, 1)),
    }
    nc = bacc.Bacc("TRN2", target_bir_lowering=False, num_devices=1)
    args = [nc.dram_tensor(k, a.shape, mybir.dt.from_np(a.dtype), kind="ExternalInput").ap() for k, a in arrays.items()]
    out = nc.dram_tensor("out", (NB, T, D), F32, kind="ExternalOutput").ap()
    decoder_layer(nc, *args, out)
    r = run_bass_kernel_spmd(nc, [arrays], core_ids=[0])
    return r.results[0]["out"]
```

```python
from contextlib import ExitStack

import concourse.bass as bass
from concourse import mybir

F32 = mybir.dt.float32
F32R = mybir.dt.float32r
U32 = mybir.dt.uint32
ALU = mybir.AluOpType
ACT = mybir.ActivationFunctionType
X = mybir.AxisListType.X

NB, T, D, NT = 8, 112, 512, 896
HT = NT // 2
KC = 4
NH, DH = 16, 128
M, MC, MS = 375, 3, 125
XH = 16
VW = 34
NE, NI, NCH = 8, 352, 28


class Queue:

    def __init__(self, name, sem):
        self.name, self.sem, self.n, self.ops, self.met = name, sem, 0, [], {}

    def needs(self, *tokens):
        for t in tokens:
            if t is None:
                continue
            if isinstance(t, list):
                self.needs(*t)
                continue
            key, sem, value = t
            if self.met.get(key, 0) < value:
                self.met[key] = value
                self.ops.append(("wait", sem, value))

    def __call__(self, fn, *tokens, inc=True):
        self.needs(*tokens)
        if inc:
            self.n += 1
            self.ops.append(("do", fn, self.sem))
            return (self.name, self.sem, self.n)
        self.ops.append(("do", fn, None))
        return None

    def load(self, fn, lane, *tokens):
        self.needs(*tokens)
        lane[2] += 16
        self.ops.append(("dma", fn, lane[1]))
        return (lane[0], lane[1], lane[2])

    def last(self):
        return (self.name, self.sem, self.n) if self.n else None

    def play(self, eng):
        for kind, a, b in self.ops:
            if kind == "wait":
                eng.wait_ge(a, b)
            elif kind == "dma":
                a(eng).then_inc(b, 16)
            elif b is None:
                a(eng)
            else:
                a(eng).then_inc(b, 1)


def decoder_layer(nc, x_d, ctx_d, wqk_d, wv_d, wo_d, wqx_d, wkv_d, gw_d, moe_d, ident_d, mask_d, iota_d, out_d):
    stack = ExitStack()
    with stack:
        place = [nc.sbuf_base + 63 & ~63]
        top = nc.sbuf_usable_end & ~31

        def sb(name, shape, dt):
            n = 4
            for s in shape[1:]:
                n *= s
            t = nc.alloc_sbuf_tensor_at(name, shape, dt, offset=place[0])
            place[0] += n + 31 & ~31
            assert place[0] <= top, (name, place[0], top)
            return t

        banks = [stack.enter_context(nc.psum_tensor(f"bank{i}", [128, 512], F32)) for i in range(8)]

        def queue(name):
            return Queue(name, stack.enter_context(nc.semaphore("q_" + name)))

        pe, act, dve, pool, sp = (queue(n) for n in ("pe", "act", "dve", "pool", "sp"))

        def lane(name):
            return [name, stack.enter_context(nc.semaphore("d_" + name)), 0]

        def mm(out, w, m, start, stop, *needs, inc=False):
            return pe(lambda e: e.matmul(out, w, m, start=start, stop=stop), *needs, inc=inc)

        def mm3(out, w, m, first, last, *needs, inc=False):
            mm(out, w[0], m[0], first, False, *needs)
            mm(out, w[1], m[0], False, False)
            return mm(out, w[0], m[1], False, last, inc=inc)

        def tr(out, in_, idn, *needs, inc=False):
            return pe(lambda e: e.transpose(out, in_, idn), *needs, inc=inc)

        def copy_act(out, in_, *needs):
            return act(lambda e: e.activation(out, in_, ACT.Copy), *needs)

        def copy_dve(out, in_, *needs):
            return dve(lambda e: e.tensor_copy(out, in_), *needs)

        def tt(q, out, a, b, op, *needs):
            return q(lambda e: e.tensor_tensor(out, a, b, op), *needs)

        def split(out, src, *needs, lo=None):
            th = copy_act(out[0], src, *needs)
            return tt(lo or dve, out[1], src, out[0].bitcast(F32), ALU.subtract, th)

        def pair(name, shape):
            return sb(name + "_hi", shape, F32R), sb(name + "_lo", shape, F32R)

        def at(p, *idx):
            return p[0].__getitem__(idx), p[1].__getitem__(idx)

        ident = sb("ident", [128, 128], F32)
        xs = sb("xs", [T, NB, D], F32)
        xT = pair("xT", [128, KC, NT])
        st = sb("st", [128, NB, 6], F32)
        mv = sb("mv", [128, NB, 2], F32)
        ve = sb("ve", [128, NB], F32)
        rstd = sb("rstd", [128, NB], F32)
        rt = [sb(f"rt{i}", [128, 16], F32) for i in range(2)]
        epsc = sb("epsc", [128, 2], F32)
        xn = [sb("xn0", [128, D], F32)]
        base = place[0]

        act(lambda e: e.preload_act_table_set("natural_log_exp_and_others"), inc=False)

        def rsqrt_start(y, v, t, *free):
            t = act(lambda e: e.activation(y, v, ACT.Ln), t, *free)
            return act(lambda e: e.activation(y, y, ACT.Exp, scale=-0.5), t)

        def rsqrt_end(y, v, tmp, t, *free):
            t = dve(lambda e: e.scalar_tensor_tensor(tmp, y, -0.5, y, ALU.mult, ALU.mult), t, *free)
            t = tt(dve, tmp, tmp, v, ALU.mult, t)
            return dve(lambda e: e.scalar_tensor_tensor(y, tmp, 1.5, y, ALU.add, ALU.mult), t)

        rt_free = [None, None]
        n_rt = [0]
        xn_use = [2]
        xn_free = [None, None]
        n_xn = [0]

        def ln_stats(rows, j, R, *needs):
            t = dve(lambda e: e.bn_stats(st[0:R, j, :], rows), *needs)
            t = dve(lambda e: e.bn_aggr(mv[0:R, j, :], st[0:R, j, :]), t)
            t = dve(lambda e: e.tensor_scalar(ve[0:R, j:j + 1], mv[0:R, j, 1:2], 1e-5, None, ALU.add), t)
            return rsqrt_start(rstd[0:R, j:j + 1], ve[0:R, j:j + 1], t)

        def ln_apply(rows, j, R, t_rstd, bank, free, x_free, at0):
            i, r = n_xn[0] % xn_use[0], n_rt[0] % 2
            n_xn[0] += 1
            n_rt[0] += 1
            t = rt_free[r] = rsqrt_end(rstd[0:R, j:j + 1], ve[0:R, j:j + 1], rt[r][0:R, 0:1], t_rstd, rt_free[r])
            t = dve(lambda e: e.tensor_scalar(xn[i][0:R, :], rows, mv[0:R, j, 0:1], rstd[0:R, j:j + 1],
                                              ALU.subtract, ALU.mult), t, xn_free[i])
            for k in range(KC):
                tp = tr(bank[:, k * R:(k + 1) * R], xn[i][0:R, k * 128:(k + 1) * 128], ident[0:R, 0:R],
                        t, t_id, free, inc=k == KC - 1)
            xn_free[i] = tp
            return split(at(xT, slice(None), slice(None), slice(at0, at0 + R)),
                         bank[:, 0:KC * R].rearrange("p (k t) -> p k t", k=KC), tp, x_free)

        NA = 7
        xa = sb("xa", [128, NA, D], F32)
        mask = sb("mask", [T, T], F32)
        xn.append(sb("xn1", [128, D], F32))
        wqk_f = [sb(f"wqk_f{i}", [128, KC, 256], F32) for i in range(2)]
        wqk = [pair(f"wqk{i}", [128, KC, 256]) for i in range(2)]
        wv_f = sb("wv_f", [128, KC, 256], F32)
        wv = pair("wv", [128, KC, 256])
        wo_f = sb("wo_f", [128, 2, D], F32)
        wo = pair("wo", [128, 2, D])
        qk = [sb(f"qk{i}", [128, 2, NT], F32) for i in range(2)]
        vv = [sb(f"vv{i}", [T, NB, 256], F32) for i in range(2)]
        sm = [sb(f"sm{i}", [T, 4, T], F32) for i in range(2)]
        pp = [sb(f"pp{i}", [T, 4, T], F32) for i in range(2)]
        pt = [sb(f"pt{i}", [T, 4 * T], F32) for i in range(2)]
        zT = pair("zT", [128, 2, NT])
        nm = [sb(f"nm{i}", [T, 4], F32) for i in range(2)]
        rs = [sb(f"rs{i}", [T, 4], F32) for i in range(2)]
        rc = [sb(f"rc{i}", [T, 4], F32) for i in range(2)]
        end_a = place[0]
        ctx = [pair(f"ctx{i}", [128, KC, MS]) for i in range(2)]
        start_p = place[0]
        assert start_p <= top - 32768
        place[0] = top - 32768
        wkv = pair("wkv", [128, KC, 2, D])

        l_x = [lane(f"x{i}") for i in range(NA)]
        l_c, l_m = lane("ident"), lane("mask")
        l_wqk = [lane("wqk0"), lane("wqk1")]
        l_wv, l_wo, l_wx = lane("wv"), lane("wo"), lane("wx")
        wqk_stage = [None, None]
        wv_stage = wo_stage = None
        PJ, SB_, TB = banks[0:4], banks[4:6], banks[6:8]
        pj_free, s_free, tb_free = [None] * 4, [None] * 2, [None] * 2
        n_pj = [0]

        def pj_next():
            i = n_pj[0] % 4
            n_pj[0] += 1
            return i

        ISQ = 1.0 / float(DH) ** 0.5

        def prep_wqk(h, free):
            i = h % 2
            t = sp.load(lambda e: e.dma_start(wqk_f[i][:, :, :], wqk_d[h]), l_wqk[i], wqk_stage[i])
            t = split(at(wqk[i], slice(None)), wqk_f[i][:, :, :], t, free, lo=pool)
            wqk_stage[i] = t
            return t

        def prep_wv(p, free):
            nonlocal wv_stage
            t = sp.load(lambda e: e.dma_start(wv_f[:, :, :], wv_d[p]), l_wv, wv_stage)
            wv_stage = split(at(wv, slice(None)), wv_f[:, :, :], t, free, lo=pool)
            return wv_stage

        def prep_wo(p, free):
            nonlocal wo_stage
            t = sp.load(lambda e: e.dma_start(wo_f[:, :, :], wo_d[p]), l_wo, wo_stage)
            wo_stage = split(at(wo, slice(None)), wo_f[:, :, :], t, free, lo=pool)
            return wo_stage

        t_wqk = [None] * NH
        t_pj = [None] * NH
        t_qk = [None] * NH
        t_sc = [None] * NH
        t_x = []
        for j in range(4):
            t_x.append(sp.load(lambda e, j=j: e.dma_start(xa[:, j, :], x_d[j]), l_x[j]))
            if j == 0:
                t_id = sp.load(lambda e: e.dma_start(ident[:, :], ident_d), l_c)
        t_xT = [None] * NA
        t_rs = {}

        def norm_first(j):
            tb_free[j % 2] = t_xT[j] = ln_apply(xa[:, j, :], j, 128, t_rs[j], TB[j % 2], tb_free[j % 2], None, 128 * j)

        t_wqk[0] = prep_wqk(0, None)
        for j in range(4, NA):
            t_x.append(sp.load(lambda e, j=j: e.dma_start(xa[:, j, :], x_d[j]), l_x[j]))
        t_wvp = prep_wv(0, None)
        for j in range(NA):
            t_rs[j] = ln_stats(xa[:, j, :], j, 128, t_x[j])
            if j >= 1:
                norm_first(j - 1)
        norm_first(NA - 1)
        t_mask = sp.load(lambda e: e.dma_start(mask[:, :], mask_d), l_m)
        t_wqk[1] = prep_wqk(1, None)
        t_wop = prep_wo(0, None)

        def project_qk(h):
            w = wqk[h % 2]
            t_done = []
            for n in range(2):
                for j in range(2):
                    i = pj_next()
                    for k in range(KC):
                        t = mm3(PJ[i][:, 0:HT], at(w, slice(None), k, slice(j * 128, j * 128 + 128)),
                                at(xT, slice(None), k, slice(n * HT, n * HT + HT)), k == 0, k == KC - 1,
                                t_wqk[h], t_xT[3 * n + 3], pj_free[i], inc=k == KC - 1)
                    f = copy_act if j else copy_dve
                    pj_free[i] = f(qk[h % 2][:, j, n * HT:n * HT + HT], PJ[i][:, 0:HT], t, t_sc[h - 2] if h >= 2 else None)
                    t_done.append(pj_free[i])
            t_pj[h] = t
            t_qk[h] = t_done

        t_av = [None] * NH
        t_v = [None] * (NH // 2)

        def project_v(p):
            t_done = []
            for b in range(0, NB, 2):
                i = pj_next()
                for c in range(2):
                    for k in range(KC):
                        t = mm3(PJ[i][0:T, c * 256:c * 256 + 256],
                                at(xT, slice(None), k, slice((b + c) * T, (b + c + 1) * T)),
                                at(wv, slice(None), k, slice(None)), k == 0, k == KC - 1,
                                t_wvp, t_xT, pj_free[i], inc=k == KC - 1)
                f = copy_act if b % 4 else copy_dve
                pj_free[i] = f(vv[p % 2][:, b:b + 2, :], PJ[i][0:T, :].rearrange("p (c n) -> p c n", c=2), t,
                               t_av[2 * p - 3] if p >= 2 else None)
                t_done.append(pj_free[i])
            t_v[p] = t_done
            return t

        t_sm = [None, None]
        t_pn = [None, None]
        t_pt_pe = [None, None]

        def scores(h):
            q = qk[h % 2]
            for g in range(2):
                for c in range(4):
                    b = 4 * g + c
                    t = mm(SB_[g][0:T, c * T:(c + 1) * T], q[:, 0, b * T:(b + 1) * T], q[:, 1, b * T:(b + 1) * T],
                           True, True, t_qk[h], s_free[g], inc=c == 3)
                t_sc[h] = t
                t = tt(dve, sm[g][:, :, :], SB_[g][0:T, 0:4 * T].rearrange("p (c t) -> p c t", c=4),
                       mask[:, :].unsqueeze(1).to_broadcast([T, 4, T]), ALU.add, t, t_mask, t_sm[g])
                s_free[g] = t
                t = dve(lambda e, g=g: e.tensor_reduce(nm[g][:, :], sm[g][:, :, :], X, ALU.max, negate=True), t)
                t = dve(lambda e, g=g: e.tensor_scalar(nm[g][:, :], nm[g][:, :], ISQ, None, ALU.mult), t)
                for c in range(4):
                    t_sm[g] = act(lambda e, g=g, c=c: e.activation(
                        pp[g][:, c, :], sm[g][:, c, :], ACT.Exp, bias=nm[g][:, c:c + 1], scale=ISQ,
                        accum_out=rs[g][:, c:c + 1]), t, t_pt_pe[g])

        def normalise(h):
            for g in range(2):
                t = dve(lambda e, g=g: e.reciprocal(rc[g][:, :], rs[g][:, :]), t_sm[g])
                t_pn[g] = tt(dve, pp[g][:, :, :], pp[g][:, :, :],
                             rc[g][:, :].unsqueeze(2).to_broadcast([T, 4, T]), ALU.mult, t)

        t_pt = [None, None]

        def transpose_p(h):
            for g in range(2):
                for c in range(4):
                    t = tr(TB[g][0:T, c * T:(c + 1) * T], pp[g][:, c, :], ident[0:T, 0:T], t_pn[g], tb_free[g],
                           inc=c == 3)
                t_pt_pe[g] = t
                f = copy_act if g else copy_dve
                tb_free[g] = t_pt[g] = f(pt[g][:, :], TB[g][0:T, 0:4 * T], t, t_av[h - 1] if h else None)

        t_wo_pe = None
        t_z = None

        def weighted_v(h):
            nonlocal t_z
            o = (h % 2) * 128
            t_done = [t_z]
            for g in range(2):
                i = pj_next()
                for c in range(4):
                    t = mm(PJ[i][:, c * T:(c + 1) * T], vv[h // 2 % 2][:, 4 * g + c, o:o + 128],
                           pt[g][:, c * T:(c + 1) * T], True, True, t_pt[g], t_v[h // 2], pj_free[i], inc=c == 3)
                pj_free[i] = split(at(zT, slice(None), h % 2, slice(g * HT, g * HT + HT)), PJ[i][:, 0:HT], t, t_wo_pe)
            t_av[h] = t
            t_z = pj_free[i]

        t_res = list(t_x)

        def project_o(p):
            nonlocal t_wo_pe
            for j in range(NA):
                i = pj_next()
                for c in range(2):
                    t = mm3(PJ[i][:, :], at(zT, slice(None), c, slice(j * 128, (j + 1) * 128)),
                            at(wo, slice(None), c, slice(None)), c == 0, c == 1, t_z, t_wop, pj_free[i], inc=c == 1)
                pj_free[i] = t_res[j] = tt(dve, xa[:, j, :], xa[:, j, :], PJ[i][:, :], ALU.add, t, t_res[j])
            t_wo_pe = t

        t_wkv = []

        def prep_wkv(k, stage):
            t = sp.load(lambda e: e.dma_start(wv_f[:, :, :].rearrange("p a n -> p (a n)"),
                                              wkv_d[:, k * 1024:(k + 1) * 1024]), l_wx, stage)
            t_wkv.append(split(at(wkv, slice(None), k), wv_f[:, :, :].rearrange("p (a b) n -> p a (b n)", a=2),
                               t, lo=pool))

        l_cx = [lane("cx0"), lane("cx1")]
        t_ctx = {}

        project_qk(0)
        t_vpe = project_v(0)
        scores(0)
        normalise(0)
        for h in range(NH):
            if h + 1 < NH:
                project_qk(h + 1)
            if h + 2 < NH:
                t_wqk[h + 2] = prep_wqk(h + 2, t_pj[h])
            if h % 2 == 0 and h + 2 < NH:
                t_wvp = prep_wv(h // 2 + 1, t_vpe)
            if h >= 13:
                prep_wkv(h - 13, t_wkv[-1] if t_wkv else wv_stage)
            transpose_p(h)
            if h + 1 < NH:
                scores(h + 1)
            weighted_v(h)
            if h + 1 < NH:
                normalise(h + 1)
            if h == NH - 1:
                prep_wkv(3, t_wkv[-1])
                for m in range(2):
                    f = wo_f[:, :, :].rearrange("p a n -> p (a n)")[:, m * 512:m * 512 + 500]
                    t = sp.load(lambda e, f=f, m=m: e.dma_start(f, ctx_d[0, m].rearrange("p a n -> p (a n)")),
                                l_cx[m], wo_stage)
                    t_ctx[0, m] = split(at(ctx[m], slice(None)), f.rearrange("p (a n) -> p a n", a=KC), t, lo=pool)
            if h % 2:
                if h + 1 < NH:
                    t_vpe = project_v(h // 2 + 1)
                project_o(h // 2)
                if h + 1 < NH:
                    t_wop = prep_wo(h // 2 + 1, t_wo_pe)

        l_r = [lane(f"r{b}") for b in range(NB)]
        t_rows = []
        for b in range(NB):
            r = 0
            while r < T:
                j, p = (b * T + r) // 128, (b * T + r) % 128
                n = min(T - r, 128 - p)
                t = sp.load(lambda e, b=b, r=r, j=j, p=p, n=n: e.dma_start(xs[r:r + n, b, :], xa[p:p + n, j, :]),
                            l_r[b], t_res[j])
                r += n
            t_rows.append(t)

        done_a = [q.last() for q in (pe, act, dve, pool)]
        xn_use[0] = 1

        NU = 2 * NB
        place[0] = start_p

        def sbl(name, shape, dt):
            n = 4
            for s in shape[1:]:
                n *= s
            n = n + 31 & ~31
            for region in regions:
                if region[0] + n <= region[1]:
                    t = nc.alloc_sbuf_tensor_at(name, shape, dt, offset=region[0])
                    region[0] += n
                    return t
            raise AssertionError((name, regions))

        regions = [[base, base + NA * D * 4]]
        ep = []
        for i in range(4):
            ep.append((sbl(f"ep{i}_hi", [MS, 4 * T], F32R), sbl(f"ep{i}_lo", [MS, 4 * T], F32R)))
        regions = [[base + NA * D * 4, end_a], [start_p, top - 32768]]

        def pairl(name, shape):
            return sbl(name + "_hi", shape, F32R), sbl(name + "_lo", shape, F32R)

        kT = [sbl(f"kT{i}", [128, 8, M], F32R) for i in range(2)]
        qT = [sbl(f"qT{i}", [128, 8, 2, T], F32R) for i in range(2)]
        wqx = pairl("wqx", [128, KC, D])
        vb = [sbl(f"vb{i}", [MS, MC, XH, VW], F32R) for i in range(2)]
        kk = [sbl(f"kk{i}", [MS, XH, 4, 16], F32R) for i in range(2)]
        ctx += [pairl(f"ctx{i}", [128, KC, MS]) for i in (2, 3)]
        ctx_f = [sbl(f"ctx_f{i}", [128, KC, MS], F32) for i in range(2)]
        wx_f = sbl("wx_f", [128, 256], F32)
        ee = [sbl(f"ee{i}", [MS, 4 * T], F32) for i in range(2)]
        ep += [pairl(f"ep{i}", [MS, 4 * T]) for i in (4, 5)]
        oo = [sbl(f"oo{i}", [VW, 4 * T], F32) for i in range(2)]
        sq = [sbl(f"sq{i}", [MS, 256], F32) for i in range(2)]
        kn = [sbl(f"kn{i}", [MS, 256], F32) for i in range(2)]
        ss = [sbl(f"ss{i}", [MS, XH], F32) for i in range(2)]
        rr = [sbl(f"rr{i}", [MS, XH], F32) for i in range(2)]
        rq = [sbl(f"rq{i}", [MS, XH], F32) for i in range(2)]
        zz = sbl("zz", [T, 4, 16], F32)
        zc = sbl("zc", [T, 4], F32)
        gw_f = sbl("gw_f", [128, KC, NE], F32)
        gw = pairl("gw", [128, KC, NE])
        pr = sbl("pr", [T, NE], F32)
        r1 = sbl("r1", [T, 4], F32)
        mx8 = sbl("mx8", [T, 8], F32)
        ix8 = sbl("ix8", [T, 8], U32)
        ixf = sbl("ixf", [T, 8], F32)
        w2 = sbl("w2", [T, 2], F32)
        cm0 = sbl("cm0", [T, NE], F32)
        cm1 = sbl("cm1", [T, NE], F32)
        comb = sbl("comb", [T, NB, NE], F32)
        iot = sbl("iot", [T, NE], F32)

        t_wqx = []
        t = None
        for k in range(2 * KC):
            t = sp.load(lambda e, k=k: e.dma_start(wx_f[:, :], wqx_d[:, k * 256:(k + 1) * 256]), l_wx, done_a, t)
            t = split(at(wqx, slice(None), k // 2, slice(k % 2 * 256, k % 2 * 256 + 256)), wx_f[:, :], t, done_a, lo=pool)
        t_wqx = t
        t_one = None
        for i in range(2):
            pool(lambda e, i=i: e.memset(vb[i][:, :, :, 32:33].bitcast(F32), 1.0), done_a)
            t_one = pool(lambda e, i=i: e.memset(vb[i][:, :, :, 33:34].bitcast(F32), 0.0), done_a)
        t_zero = [dve(lambda e, i=i: e.memset(qT[i][:, :, :, :].bitcast(F32), 0.0), done_a) for i in range(2)]

        KB, SX, AB, TX = banks[0:2], banks[2:5], banks[5], banks[6:8]
        kb_free, sx_free, tx_free = pj_free[0:2], [pj_free[2], pj_free[3], s_free[0]], list(tb_free)
        ab_free = s_free[1]
        n_kb, n_sx, n_tx, n_ep = [0], [0], [0], [0]

        def turn(c, n):
            i = c[0] % n
            c[0] += 1
            return i

        ctx_stage = [done_a, done_a]
        ctx_use = [None, None, done_a, done_a]

        def load_ctx(b, m):
            n = b * MC + m
            if b >= NB:
                return
            i, j = n % 2, n % 4
            t = sp.load(lambda e: e.dma_start(ctx_f[i][:, :, :], ctx_d[b, m]), l_cx[i], ctx_stage[i])
            ctx_stage[i] = t_ctx[b, m] = split(at(ctx[j], slice(None)), ctx_f[i][:, :, :], t, ctx_use[j], lo=pool)

        vb_free, kT_free, qT_free = [done_a] * 2, [done_a] * 2, [done_a] * 2
        sq_free, kn_free, kk_free = [done_a] * 2, [done_a] * 2, [done_a] * 2
        t_kT, t_qT, t_vb = [None] * NU, [None] * NU, [None] * NU
        rows = {}
        n_row = [0]

        def rms(i, src, R, t):
            t_sq = t = act(lambda e: e.activation(sq[i][0:R, :], src, ACT.Square), t, sq_free[i])
            t = dve(lambda e: e.tensor_reduce(ss[i][0:R, :], sq[i][0:R, :].rearrange("p (h d) -> p h d", d=16),
                                              X, ALU.add), t, kn_free[i])
            sq_free[i] = t
            return t_sq, dve(lambda e: e.tensor_scalar(ss[i][0:R, :], ss[i][0:R, :], 1.0 / 16, 1e-6, ALU.mult, ALU.add), t)

        def kv_rows(u, m):
            if u >= NU:
                return
            b, hf = u // 2, u % 2
            j = (b * MC + m) % 4
            i = turn(n_kb, 2)
            for k in range(KC):
                t = mm3(KB[i][0:MS, :], at(ctx[j], slice(None), k, slice(None)),
                        at(wkv, slice(None), k, hf, slice(None)), k == 0, k == KC - 1,
                        t_ctx[b, m], t_wkv, kb_free[i], inc=k == KC - 1)
            ctx_use[j] = t
            r = turn(n_row, 2)
            src = KB[i][0:MS, 0:256]
            t_sq, t_r = rms(r, src, MS, t)
            v = KB[i][0:MS, 256:512].rearrange("p (h d) -> p h d", d=16)
            vh, vl = vb[u % 2][:, m, :, 0:16], vb[u % 2][:, m, :, 16:32]
            t = copy_act(vh, v, t, vb_free[u % 2], t_one)
            t_r = rsqrt_start(rr[r][0:MS, :], ss[r][0:MS, :], t_r)
            t_vb[u] = tt(dve, vl, v, vh.bitcast(F32), ALU.subtract, t, vb_free[u % 2])
            rows[u, m] = (i, r, src, MS, [t_sq, t_r, t_vb[u]])
            if hf and m < 2:
                load_ctx(b + 1, m + 1)
            if hf and m == 2:
                load_ctx(b + 2, 0)

        def q_rows(u):
            if u >= NU:
                return
            b, hf = u // 2, u % 2
            i = turn(n_kb, 2)
            for k in range(KC):
                t = mm3(KB[i][0:T, 0:256], at(xT, slice(None), k, slice(b * T, (b + 1) * T)),
                        at(wqx, slice(None), k, slice(hf * 256, hf * 256 + 256)), k == 0, k == KC - 1,
                        t_xT2[b], t_wqx, kb_free[i], inc=k == KC - 1)
            t_q_pe[b] = t
            r = turn(n_row, 2)
            t_sq, t_r = rms(r, KB[i][0:T, 0:256], T, t)
            t_r = rsqrt_start(rr[r][0:T, :], ss[r][0:T, :], t_r)
            rows[u, "q"] = (i, r, KB[i][0:T, 0:256], T, [t_sq, t_r])

        def finish_rows(u, m):
            if u >= NU:
                return
            i, r, src, R, t = rows.pop((u, m))
            t = rsqrt_end(rr[r][0:R, :], ss[r][0:R, :], rq[r][0:R, :], t)
            t = tt(dve, kn[r][0:R, :].rearrange("p (h d) -> p h d", d=16), src.rearrange("p (h d) -> p h d", d=16),
                   rr[r][0:R, :].unsqueeze(2).to_broadcast([R, XH, 16]), ALU.mult, t, kn_free[r])
            kb_free[i] = t
            row = kn[r][0:R, :].rearrange("p (h d) -> p h d", d=16)
            twice = row.unsqueeze(2).to_broadcast([R, XH, 2, 16])
            o = kk[r][0:R, :, :, :]
            if m == "q":
                hi, lo, first = o[:, :, 0:2, :], o[:, :, 2:4, :], o[:, :, 0, :]
            else:
                o = o.rearrange("p h (a c) d -> p h a c d", c=2)
                hi, lo, first = o[:, :, :, 0, :], o[:, :, :, 1, :], kk[r][0:R, :, 0, :]
            t = copy_dve(hi, twice, t, kk_free[r])
            first2 = first.bitcast(F32).unsqueeze(2).to_broadcast([R, XH, 2, 16])
            t = tt(dve, lo, twice, first2, ALU.subtract, t)
            kn_free[r] = t
            rows[u, m] = (r, R, t)

        def turn_rows(u, m):
            if u >= NU:
                return
            r, R, t = rows.pop((u, m))
            s = kk[r][0:R, :, :, :].bitcast(F32).rearrange("p (g h) a d -> p g (h a d)", h=2)
            for c in range(2):
                i = turn(n_tx, 2)
                for g in range(4):
                    tp = tr(TX[i][:, g * R:(g + 1) * R], s[:, 4 * c + g, :], ident[0:R, 0:R], t, tx_free[i], inc=g == 3)
                src = TX[i][:, 0:4 * R].rearrange("p (g t) -> p g t", g=4)
                if m == "q":
                    for o in range(2):
                        tx_free[i] = copy_act(qT[u % 2][64 * o:64 * o + 64, 4 * c:4 * c + 4, o, :],
                                              src[64 * o:64 * o + 64], tp, qT_free[u % 2], t_zero)
                    t_qT[u] = tx_free[i]
                else:
                    tx_free[i] = copy_act(kT[u % 2][:, 4 * c:4 * c + 4, m * MS:(m + 1) * MS], src, tp, kT_free[u % 2])
                    t_kT[u] = tx_free[i]
            kk_free[r] = tp

        ee_free, ep_free = [done_a] * 2, [done_a + t_rows] * 6
        oo_free = [done_a] * 2
        probs = {}
        outs = {}
        n_ee = [0]
        n_oo = [0]

        def score_quad(u, q):
            if u >= NU:
                return
            for m in range(MC):
                i = turn(n_sx, 3)
                for c in range(2):
                    t = mm(SX[i][0:MS, c * 2 * T:(c + 1) * 2 * T], kT[u % 2][:, 2 * q + c, m * MS:(m + 1) * MS],
                           qT[u % 2][:, 2 * q + c, :, :], True, True, t_kT[u], t_qT[u], sx_free[i], inc=c == 1)
                if m == MC - 1 and q == 3:
                    kT_free[u % 2] = qT_free[u % 2] = t
                e, p = turn(n_ee, 2), turn(n_ep, 6)
                t = act(lambda en, e=e, i=i: en.activation(ee[e][:, :], SX[i][0:MS, 0:4 * T], ACT.Exp, scale=0.25),
                        t, ee_free[e])
                sx_free[i] = t
                t = copy_dve(ep[p][0][:, :], ee[e][:, :], t, ep_free[p])
                t = tt(pool if m in LO_POOL else dve, ep[p][1][:, :], ee[e][:, :], ep[p][0][:, :].bitcast(F32),
                       ALU.subtract, t, ep_free[p])
                ee_free[e] = t
                probs[u, q, m] = (p, t)

        LO_POOL = (1,)

        def value_quad(u, q):
            nonlocal ab_free
            for c in range(4):
                for m in range(MC):
                    p, t = probs[u, q, m]
                    w = vb[u % 2][:, m, 4 * q + c, :]
                    o = AB[0:VW, c * T:(c + 1) * T]
                    mm(o, w, ep[p][0][:, c * T:(c + 1) * T], m == 0, False, t, t_vb[u], t_one, ab_free)
                    t = mm(o, w, ep[p][1][:, c * T:(c + 1) * T], False, m == MC - 1, inc=c == 3)
                    if c == 3:
                        ep_free[p] = t
            if q == 3:
                vb_free[u % 2] = t
            i = turn(n_oo, 2)
            ab_free = copy_act(oo[i][:, :], AB[0:VW, 0:4 * T], t, oo_free[i])
            outs[u, q] = (i, ab_free)

        t_zz = done_a
        t_row2 = list(t_rows)

        def out_quad(u, q):
            nonlocal t_zz
            b, hf = u // 2, u % 2
            i, t = outs.pop((u, q))
            j = turn(n_tx, 2)
            for c in range(4):
                tp = tr(TX[j][0:T, c * VW:(c + 1) * VW], oo[i][:, c * T:(c + 1) * T], ident[0:VW, 0:VW], t,
                        tx_free[j], inc=c == 3)
            oo_free[i] = tp
            o = TX[j][0:T, 0:4 * VW].rearrange("p (c w) -> p c w", w=VW)
            t0 = dve(lambda e: e.reciprocal(zc[:, :], o[:, :, 32]), tp, t_zz)
            t1 = dve(lambda e: e.tensor_reduce(zz[:, :, :], o[:, :, 0:32].rearrange("p c (a d) -> p c d a", a=2),
                                               X, ALU.add), tp, t_zz)
            tx_free[j] = t1
            t = tt(dve, zz[:, :, :], zz[:, :, :], zc[:, :].unsqueeze(2).to_broadcast([T, 4, 16]), ALU.mult, t0, t1)
            n = (hf * XH + 4 * q) * 16
            t_zz = t_row2[b] = tt(dve, xs[:, b, n:n + 64].rearrange("p (c d) -> p c d", d=16),
                                  xs[:, b, n:n + 64].rearrange("p (c d) -> p c d", d=16), zz[:, :, :], ALU.add,
                                  t, t_row2[b], t_ln[b])

        t_ln = [None] * NB
        t_xT2, t_xT3, t_comb = [None] * NB, [None] * NB, [None] * NB
        t_q_pe = [None] * NB
        t_rt = done_a
        t_n2, t_n3 = {}, {}

        def second_norm(b, part):
            if b >= NB:
                return
            if part == 0:
                t_n2[b] = ln_stats(xs[:, b, :], b, T, t_rows[b], t_xa)
            else:
                j = turn(n_tx, 2)
                tx_free[j] = t_xT2[b] = ln_apply(xs[:, b, :], b, T, t_n2[b], TX[j], tx_free[j], done_a, b * T)
                t_ln[b] = t_xT2[b]

        def third_norm(b, part):
            if b < 0:
                return
            if part == 0:
                t_n3[b] = ln_stats(xs[:, b, :], b, T, t_row2[b])
            else:
                j = turn(n_tx, 2)
                tx_free[j] = t_xT3[b] = ln_apply(xs[:, b, :], b, T, t_n3[b], TX[j], tx_free[j], t_q_pe[b], b * T)

        t_xa = t_xT[NA - 1]
        load_ctx(0, 2)
        load_ctx(1, 0)
        kv_rows(0, 0)
        second_norm(0, 0)
        finish_rows(0, 0)
        kv_rows(0, 1)
        second_norm(0, 1)
        turn_rows(0, 0)
        finish_rows(0, 1)
        kv_rows(0, 2)
        turn_rows(0, 1)
        finish_rows(0, 2)
        q_rows(0)
        turn_rows(0, 2)
        finish_rows(0, "q")
        kv_rows(1, 0)
        turn_rows(0, "q")
        finish_rows(1, 0)
        score_quad(0, 0)
        t = sp.load(lambda e: e.dma_start(gw_f[:, :, :], gw_d), l_wx, t_wqx)
        t_iot = sp.load(lambda e: e.dma_start(iot[:, :], iota_d), l_wx)
        t_gw = split(at(gw, slice(None)), gw_f[:, :, :], t_iot, done_a, lo=pool)
        for u in range(NU):
            n = u + 1
            b, hf = u // 2, u % 2
            score_quad(u, 1)
            q_rows(n)
            turn_rows(n, 0)
            value_quad(u, 0)
            finish_rows(n, "q")
            score_quad(u, 2)
            kv_rows(n, 1)
            value_quad(u, 1)
            out_quad(u, 0)
            if hf == 0:
                third_norm(b - 1, 0)
            finish_rows(n, 1)
            turn_rows(n, "q")
            score_quad(u, 3)
            kv_rows(n, 2)
            value_quad(u, 2)
            out_quad(u, 1)
            if hf == 0:
                second_norm(b + 1, 0)
            finish_rows(n, 2)
            turn_rows(n, 1)
            value_quad(u, 3)
            out_quad(u, 2)
            if hf == 0:
                third_norm(b - 1, 1)
                second_norm(b + 1, 1)
            turn_rows(n, 2)
            kv_rows(n + 1, 0)
            out_quad(u, 3)
            score_quad(n, 0)
            finish_rows(n + 1, 0)
        third_norm(NB - 1, 0)
        third_norm(NB - 1, 1)

        def route(b):
            nonlocal t_rt
            i = turn(n_kb, 2)
            for k in range(KC):
                t = mm3(KB[i][0:T, 0:NE], at(xT, slice(None), k, slice(b * T, (b + 1) * T)),
                        at(gw, slice(None), k, slice(None)), k == 0, k == KC - 1, t_xT3[b], t_gw, kb_free[i],
                        inc=k == KC - 1)
            l = KB[i][0:T, 0:NE]
            t = dve(lambda e: e.tensor_reduce(r1[:, 0:1], l, X, ALU.max, negate=True), t, t_rt)
            t = act(lambda e: e.activation(pr[:, :], l, ACT.Exp, bias=r1[:, 0:1], accum_out=r1[:, 1:2]), t)
            kb_free[i] = t
            t = dve(lambda e: e.reciprocal(r1[:, 2:3], r1[:, 1:2]), t)
            t = dve(lambda e: e.tensor_scalar(pr[:, :], pr[:, :], r1[:, 2:3], None, ALU.mult), t)
            t = dve(lambda e: e.max(mx8[:, :], pr[:, :]), t)
            t0 = dve(lambda e: e.max_index(ix8[:, :], mx8[:, :], pr[:, :]), t)
            t0 = copy_dve(ixf[:, :], ix8[:, :], t0)
            t = tt(dve, r1[:, 3:4], mx8[:, 0:1], mx8[:, 1:2], ALU.add, t)
            t = dve(lambda e: e.tensor_scalar(r1[:, 3:4], r1[:, 3:4], 1e-20, None, ALU.add), t)
            t = dve(lambda e: e.reciprocal(r1[:, 3:4], r1[:, 3:4]), t)
            t = dve(lambda e: e.tensor_scalar(w2[:, :], mx8[:, 0:2], r1[:, 3:4], None, ALU.mult), t)
            ta = dve(lambda e: e.tensor_scalar(cm0[:, :], iot[:, :], ixf[:, 0:1], w2[:, 0:1], ALU.is_equal, ALU.mult),
                     t, t0, t_iot)
            tb = dve(lambda e: e.tensor_scalar(cm1[:, :], iot[:, :], ixf[:, 1:2], w2[:, 1:2], ALU.is_equal, ALU.mult),
                     t, t0)
            t_rt = t_comb[b] = tt(dve, comb[:, b, :], cm0[:, :], cm1[:, :], ALU.add, ta, tb)

        for b in range(NB):
            route(b)

        done_b = [q.last() for q in (pe, act, dve, pool)]

        place[0] = base
        bc = sb("bc", [128, NE, NT], F32)
        we_f = [sb(f"we_f{i}", [128, 1536], F32) for i in range(2)]
        sg = [sb(f"sg{i}", [128, HT], F32) for i in range(2)]
        hh = [sb(f"hh{i}", [128, HT], F32) for i in range(2)]
        hs = [pair(f"hs{i}", [128, HT]) for i in range(2)]
        yo = [sb(f"yo{i}", [T, D], F32) for i in range(2)]
        cmc = sb("cmc", [T, NB, NE], F32)
        we = [pair(f"we{i}", [128, 1536]) for i in range(4)]

        AC, GU = banks[0:4], banks[4:8]
        ac_free, gu_free = [done_b] * 4, [done_b] * 4
        n_gu = [0]
        t_cmc = copy_dve(cmc[:, :, :], comb[:, :, :], done_b)
        for e_ in range(NE):
            for n in range(2):
                i = turn(n_gu, 4)
                for c in range(4):
                    b = 4 * n + c
                    t = mm(GU[i][:, c * T:(c + 1) * T], cmc[:, b, e_:e_ + 1].to_broadcast([T, 128]), ident[0:T, 0:T],
                           True, True, t_cmc, gu_free[i], inc=c == 3)
                gu_free[i] = t_bc = copy_act(bc[:, e_, n * HT:(n + 1) * HT], GU[i][:, 0:HT], t)

        l_we = [lane("we0"), lane("we1")]
        l_out = [lane("out0"), lane("out1")]
        we_stage = [done_b, done_b]
        we_free = [done_b] * 4
        t_bcs = act.last()

        def load_chunk(s):
            c = s % NCH
            i, j = s % 2, s % 4
            t = sp.load(lambda e: e.dma_start(we_f[i][:, :], moe_d[c]), l_we[i], we_stage[i])
            t = copy_act(we[j][0][:, :], we_f[i][:, :], t, we_free[j])
            we_stage[i] = tt(pool, we[j][1][:, :], we_f[i][:, :], we[j][0][:, :].bitcast(F32), ALU.subtract, t)
            return we_stage[i]

        sg_free, hh_free, hs_free = [done_b] * 2, [done_b] * 2, [done_b] * 2
        yo_free = [done_b] * 2
        t_we = {i: load_chunk(i) for i in range(3)}
        t_hs = {}

        def up(s):
            n, c, w = s // NCH, s % NCH, we[s % 4]
            i = [turn(n_gu, 4), turn(n_gu, 4)]
            tg = []
            for a in range(2):
                for k in range(KC):
                    o = k * 256 + a * 128
                    t = mm3(GU[i[a]][:, 0:HT], at(w, slice(None), slice(o, o + 128)),
                            at(xT, slice(None), k, slice(n * HT, n * HT + HT)), k == 0, k == KC - 1,
                            t_we[s], t_xT3, gu_free[i[a]], inc=k == KC - 1)
                tg.append(t)
            j = s % 2
            t = act(lambda e: e.activation(sg[j][:, :], GU[i[0]][:, 0:HT], ACT.Silu), tg[0], sg_free[j])
            gu_free[i[0]] = t
            t = tt(dve, hh[j][:, :], sg[j][:, :], GU[i[1]][:, 0:HT], ALU.mult, t, tg[1], hh_free[j])
            gu_free[i[1]] = sg_free[j] = t
            r = 0
            while r < 128 and c * 128 + r < NE * NI:
                x_ = (c * 128 + r) // NI
                z = min(128, (x_ + 1) * NI - c * 128)
                z = min(z, r + 32 if r in (32, 96) else r + 64 if r == 64 else 128)
                tm = tt(dve, hh[j][r:z, :], hh[j][r:z, :], bc[r:z, x_, n * HT:(n + 1) * HT], ALU.mult, t, t_bcs)
                r = z
            t = [t, dve.last()]
            hh_free[j] = t_hs[s] = split(at(hs[j], slice(None), slice(None)), hh[j][:, :], t, hs_free[j])

        t_end = []

        def down(s):
            n, c, w = s // NCH, s % NCH, we[s % 4]
            j = s % 2
            for b in range(4):
                t = mm3(AC[b][0:T, :], at(hs[j], slice(None), slice(b * T, (b + 1) * T)),
                        at(w, slice(None), slice(1024, 1536)), c == 0, c == NCH - 1, t_hs[s], ac_free[b], inc=True)
                if c == NCH - 1:
                    y = b % 2
                    bb = 4 * n + b
                    ac_free[b] = tt(dve, yo[y][:, :], xs[:, bb, :], AC[b][0:T, :], ALU.add, t, yo_free[y])
                    yo_free[y] = sp.load(lambda e, y=y, bb=bb: e.dma_start(out_d[bb], yo[y][:, :]), l_out[y], ac_free[b])
                    t_end.append(yo_free[y])
            hs_free[j] = t
            we_free[s % 4] = t

        for s in range(2 * NCH + 1):
            if s < 2 * NCH:
                up(s)
            if s >= 1:
                down(s - 1)
                if s + 2 < 2 * NCH:
                    t_we[s + 2] = load_chunk(s + 2)
        sp.needs(*t_end)

        with nc.Block() as block:
            block.sync(sp.play)
            block.gpsimd(pool.play)
            block.scalar(act.play)
            block.vector(dve.play)
            block.tensor(pe.play)


def kernel(x, ctx_2048, L0_attn_W_K, L0_attn_W_Q, L0_attn_W_V, L0_attn_W_O, L0_xattn_Wq, L0_xattn_Wk, L0_xattn_Wv,
           L0_ffn_gate_w, L0_ffn_expert_gate, L0_ffn_expert_up, L0_ffn_expert_down, L0_ffn_shared_gate,
           L0_ffn_shared_up, L0_ffn_shared_down):
    import numpy as np
    import concourse.bacc as bacc
    from concourse.bass_utils import run_bass_kernel_spmd

    def c(a):
        return np.ascontiguousarray(a)

    def inner(a):
        a = np.asarray(a)
        a = np.swapaxes(a, -1, -2)
        a = a.reshape(a.shape[:-2] + (KC, 128, a.shape[-1]))
        return np.swapaxes(a, -2, -3)

    wk, wq, wv = (np.asarray(a) for a in (L0_attn_W_K, L0_attn_W_Q, L0_attn_W_V))
    wqk = inner(np.concatenate([wq, wk], axis=1))
    wvp = inner(wv.reshape(NH // 2, 2 * DH, D))
    wo = np.asarray(L0_attn_W_O).T.reshape(NH // 2, 2, DH, D).transpose(0, 2, 1, 3)
    ctx = inner(np.asarray(ctx_2048).reshape(NB, MC, MS, D))
    wcat = np.concatenate([np.asarray(L0_xattn_Wk), np.asarray(L0_xattn_Wv)], axis=0)
    wcat = wcat.reshape(2, XH, 16, 2, D).transpose(0, 3, 1, 2, 4).reshape(2 * 512, D)
    wkv = inner(wcat).reshape(128, KC * 1024)
    wqx = inner(L0_xattn_Wq).reshape(128, KC * D)
    gw = inner(L0_ffn_gate_w)
    up = np.zeros((2, NCH * 128, D), np.float32)
    n = NE * NI
    for i, (a, b) in enumerate(((L0_ffn_expert_gate, L0_ffn_shared_gate), (L0_ffn_expert_up, L0_ffn_shared_up))):
        up[i, :n] = np.asarray(a).reshape(n, D)
        up[i, n:n + 2 * NI] = np.asarray(b)
    dn = np.zeros((NCH * 128, D), np.float32)
    dn[:n] = np.asarray(L0_ffn_expert_down).transpose(0, 2, 1).reshape(n, D)
    dn[n:n + 2 * NI] = np.asarray(L0_ffn_shared_down).T
    upc = inner(up.reshape(2, NCH, 128, D).transpose(1, 0, 2, 3).reshape(NCH, 256, D)).reshape(NCH, 128, KC * 256)
    moe = np.concatenate([upc, dn.reshape(NCH, 128, D)], axis=2)
    i = np.arange(T)
    arrays = {
        "x": c(x).reshape(7, 128, D), "ctx": c(ctx), "wqk": c(wqk), "wv": c(wvp), "wo": c(wo), "wqx": c(wqx), "wkv": c(wkv), "gw": c(gw),
        "moe": c(moe), "ident": np.eye(128, dtype=np.float32),
        "mask": np.where(i[:, None] >= i[None, :], 0.0, -1e10).astype(np.float32),
        "iota": np.tile(np.arange(NE, dtype=np.float32), (T, 1)),
    }
    nc = bacc.Bacc("TRN2", target_bir_lowering=False, num_devices=1)
    args = [nc.dram_tensor(k, a.shape, mybir.dt.from_np(a.dtype), kind="ExternalInput").ap() for k, a in arrays.items()]
    out = nc.dram_tensor("out", (NB, T, D), F32, kind="ExternalOutput").ap()
    decoder_layer(nc, *args, out)
    r = run_bass_kernel_spmd(nc, [arrays], core_ids=[0])
    return r.results[0]["out"]
```

```python
from contextlib import ExitStack

import concourse.bass as bass
from concourse import mybir

F32 = mybir.dt.float32
F32R = mybir.dt.float32r
U32 = mybir.dt.uint32
ALU = mybir.AluOpType
ACT = mybir.ActivationFunctionType
X = mybir.AxisListType.X

NB, T, D, NT = 8, 112, 512, 896
HT = NT // 2
KC = 4
NH, DH = 16, 128
M, MC, MS = 375, 3, 125
XH = 16
VW = 34
NE, NI = 8, 352
NS = 6
BS = 256
NBLK = (2 * NT + NE * (BS - 1)) // BS
IC = ((0, 128), (128, 128), (256, 96))
WE = KC * 2 * NI + 3 * D


class Queue:

    def __init__(self, name, sem):
        self.name, self.sem, self.n, self.ops, self.met = name, sem, 0, [], {}

    def needs(self, *tokens):
        for t in tokens:
            if t is None:
                continue
            if isinstance(t, list):
                self.needs(*t)
                continue
            key, sem, value = t
            if self.met.get(key, 0) < value:
                self.met[key] = value
                self.ops.append(("wait", sem, value))

    def __call__(self, fn, *tokens, inc=True):
        self.needs(*tokens)
        if inc:
            self.n += 1
            self.ops.append(("do", fn, self.sem))
            return (self.name, self.sem, self.n)
        self.ops.append(("do", fn, None))
        return None

    def load(self, fn, lane, *tokens):
        self.needs(*tokens)
        lane[2] += 16
        self.ops.append(("dma", fn, lane[1]))
        return (lane[0], lane[1], lane[2])

    def last(self):
        return (self.name, self.sem, self.n) if self.n else None

    def play(self, eng):
        for kind, a, b in self.ops:
            if kind == "wait":
                eng.wait_ge(a, b)
            elif kind == "dma":
                a(eng).then_inc(b, 16)
            elif b is None:
                a(eng)
            else:
                a(eng).then_inc(b, 1)


def decoder_layer(nc, x_d, ctx_d, wqk_d, wv_d, wo_d, wqx_d, wkv_d, gw_d, moe_d, wexp_d, ident_d, mask_d, cst_d,
                  out_d):
    stack = ExitStack()
    with stack:
        place = [nc.sbuf_base + 63 & ~63]
        top = nc.sbuf_usable_end & ~31

        def sb(name, shape, dt):
            n = 4
            for s in shape[1:]:
                n *= s
            t = nc.alloc_sbuf_tensor_at(name, shape, dt, offset=place[0])
            place[0] += n + 31 & ~31
            assert place[0] <= top, (name, place[0], top)
            return t

        banks = [stack.enter_context(nc.psum_tensor(f"bank{i}", [128, 512], F32)) for i in range(8)]

        def queue(name):
            return Queue(name, stack.enter_context(nc.semaphore("q_" + name)))

        pe, act, dve, pool, sp = (queue(n) for n in ("pe", "act", "dve", "pool", "sp"))

        def lane(name):
            return [name, stack.enter_context(nc.semaphore("d_" + name)), 0]

        def mm(out, w, m, start, stop, *needs, inc=False):
            return pe(lambda e: e.matmul(out, w, m, start=start, stop=stop), *needs, inc=inc)

        def mm3(out, w, m, first, last, *needs, inc=False):
            mm(out, w[0], m[0], first, False, *needs)
            mm(out, w[1], m[0], False, False)
            return mm(out, w[0], m[1], False, last, inc=inc)

        def tr(out, in_, idn, *needs, inc=False):
            return pe(lambda e: e.transpose(out, in_, idn), *needs, inc=inc)

        def copy_act(out, in_, *needs):
            return act(lambda e: e.activation(out, in_, ACT.Copy), *needs)

        def copy_dve(out, in_, *needs):
            return dve(lambda e: e.tensor_copy(out, in_), *needs)

        def tt(q, out, a, b, op, *needs):
            return q(lambda e: e.tensor_tensor(out, a, b, op), *needs)

        def split(out, src, *needs, lo=None):
            th = copy_act(out[0], src, *needs)
            return tt(lo or dve, out[1], src, out[0].bitcast(F32), ALU.subtract, th)

        def pair(name, shape):
            return sb(name + "_hi", shape, F32R), sb(name + "_lo", shape, F32R)

        def at(p, *idx):
            return p[0].__getitem__(idx), p[1].__getitem__(idx)

        ident = sb("ident", [128, 128], F32)
        xs = sb("xs", [T, NB, D], F32)
        xT = pair("xT", [128, KC, NT])
        st = sb("st", [128, NB, 6], F32)
        mv = sb("mv", [128, NB, 2], F32)
        rstd = sb("rstd", [128, NB], F32)
        rt = [sb(f"rt{i}", [128, 16], F32) for i in range(2)]
        epsc = sb("epsc", [128, 2], F32)
        xn = [sb("xn0", [128, D], F32)]
        zt = sb("zt", [128, 128], F32)
        w01 = sb("w01", [T, 2, NB], F32)
        slot = sb("slot", [T, 2, NB], U32)
        eid = sb("eid", [1, NBLK], U32)
        base = place[0]
        slots_d = nc.dram_tensor("slots", (NBLK * BS, D), F32).ap()
        y_d = nc.dram_tensor("slots_out", (NBLK * BS, D), F32).ap()

        def exp_table():
            act(lambda e: e.preload_act_table_set("natural_log_exp_and_others"), inc=False)

        exp_table()

        EPS = 1e-5
        t_eps1 = pool(lambda e: e.memset(epsc[:, 1:2], EPS))

        def rsqrt_start(j, R, t):
            y = rstd[0:R, j:j + 1]
            t = act(lambda e: e.activation(y, mv[0:R, j, 1:2], ACT.Ln, bias=epsc[0:R, 1:2]), t, t_eps1)
            return act(lambda e: e.activation(y, y, ACT.Exp, scale=-0.5), t)

        def rsqrt_end(j, R, t, between=()):
            r = n_rt[0] % 2
            n_rt[0] += 1
            y, tmp = rstd[0:R, j:j + 1], rt[r][0:R, 0:1]
            t = dve(lambda e: e.scalar_tensor_tensor(tmp, y, -0.5, y, ALU.mult, ALU.mult), t, rt_free[r])
            for go in between:
                go()
            t = dve(lambda e: e.scalar_tensor_tensor(tmp, mv[0:R, j, 1:2], EPS, tmp, ALU.add, ALU.mult), t)
            t = rt_free[r] = dve(lambda e: e.scalar_tensor_tensor(y, tmp, 1.5, y, ALU.add, ALU.mult), t)
            return t

        rt_free = [None, None]
        n_rt = [0]
        xn_use = [2]
        xn_free = [None, None]
        n_xn = [0]

        def ln_stats(rows, j, R, *needs):
            t = dve(lambda e: e.bn_stats(st[0:R, j, :], rows), *needs)
            return dve(lambda e: e.bn_aggr(mv[0:R, j, :], st[0:R, j, :]), t)

        def ln_scale(rows, j, R, t_rstd, between=()):
            i = n_xn[0] % xn_use[0]
            n_xn[0] += 1
            t = rsqrt_end(j, R, t_rstd, between)
            return i, dve(lambda e: e.tensor_scalar(xn[i][0:R, :], rows, mv[0:R, j, 0:1], rstd[0:R, j:j + 1],
                                                    ALU.subtract, ALU.mult), t, xn_free[i])

        def ln_turn(i, t, R, bank, free, x_free, at0):
            for k in range(KC):
                tp = tr(bank[:, k * R:(k + 1) * R], xn[i][0:R, k * 128:(k + 1) * 128], ident[0:R, 0:R],
                        t, t_id, free, inc=k == KC - 1)
            xn_free[i] = tp
            to = at(xT, slice(None), slice(None), slice(at0, at0 + R))
            src = bank[:, 0:KC * R].rearrange("p (k t) -> p k t", k=KC)
            return to, src, copy_act(to[0], src, tp, x_free)

        def ln_rest(to, src, t):
            return tt(dve, to[1], src, to[0].bitcast(F32), ALU.subtract, t)

        NA = 7
        xa = sb("xa", [128, NA, D], F32)
        mask = sb("mask", [T, T], F32)
        xn.append(sb("xn1", [128, D], F32))
        place_f = place[0]
        wqk_f = [sb(f"wqk_f{i}", [128, KC, 256], F32) for i in range(2)]
        wqx_f = nc.alloc_sbuf_tensor_at("wqx_f", [128, KC, D], F32, offset=place_f)
        place_w = place[0]
        wqk = [pair(f"wqk{i}", [128, KC, 256]) for i in range(2)]
        wqx = [nc.alloc_sbuf_tensor_at(f"wqx{i}", [128, KC, D], F32R, offset=place_w + i * KC * D * 4) for i in range(2)]
        wv_f = sb("wv_f", [128, KC, 256], F32)
        wv = pair("wv", [128, KC, 256])
        place_wo = place[0]
        wo_f = sb("wo_f", [128, 2, D], F32)
        ctx_f = [nc.alloc_sbuf_tensor_at(f"ctx_f{i}", [128, KC, MS], F32, offset=place_wo + i * 2048) for i in range(2)]
        place_w2 = place[0]
        wo = pair("wo", [128, 2, D])
        place_qk = place[0]
        qk = [sb(f"qk{i}", [128, 2, NT], F32) for i in range(2)]
        vv = [sb(f"vv{i}", [T, NB, 256], F32) for i in range(2)]
        sm = [sb(f"sm{i}", [T, 4, T], F32) for i in range(2)]
        pp = [sb(f"pp{i}", [T, 4, T], F32) for i in range(2)]
        pt = [sb(f"pt{i}", [T, 4 * T], F32) for i in range(2)]
        place_z = place[0]
        zT = pair("zT", [128, 2, NT])
        place_z2 = place[0]
        nm = [sb(f"nm{i}", [T, 4], F32) for i in range(2)]
        rs = [sb(f"rs{i}", [T, 4], F32) for i in range(2)]
        rc = [sb(f"rc{i}", [T, 4], F32) for i in range(2)]
        end_a = place[0]
        ctx = [pair(f"ctx{i}", [128, KC, MS]) for i in range(2)]
        start_p = place[0]
        assert start_p <= top - 32768
        place[0] = top - 32768
        wkv = pair("wkv", [128, KC, 2, D])

        l_x = [lane(f"x{i}") for i in range(NA)]
        l_c, l_m = lane("ident"), lane("mask")
        l_wqk = [lane("wqk0"), lane("wqk1")]
        l_wv, l_wo, l_wx, l_wq, l_g, l_z = (lane(n) for n in ("wv", "wo", "wx", "wq", "g", "z"))
        wqk_stage = [None, None]
        wv_stage = wo_stage = None
        PJ, SB_, TB = banks[0:6], banks[4:6], banks[6:8]
        pj_free, s_free, tb_free = [None] * 6, [None] * 2, [None] * 2
        n_pj = [0]

        pj_use = [0, 1, 2, 3]

        def pj_next():
            i = pj_use[n_pj[0] % len(pj_use)]
            n_pj[0] += 1
            return i

        ISQ = 1.0 / float(DH) ** 0.5

        def prep_wqk(h, free):
            i = h % 2
            t = sp.load(lambda e: e.dma_start(wqk_f[i][:, :, :], wqk_d[h]), l_wqk[i], wqk_stage[i])
            t = split(at(wqk[i], slice(None)), wqk_f[i][:, :, :], t, free, lo=pool)
            wqk_stage[i] = t
            return t

        def prep_wv(p, free):
            nonlocal wv_stage
            t = sp.load(lambda e: e.dma_start(wv_f[:, :, :], wv_d[p]), l_wv, wv_stage)
            wv_stage = split(at(wv, slice(None)), wv_f[:, :, :], t, free, lo=pool)
            return wv_stage

        def prep_wo(p, free):
            nonlocal wo_stage
            t = sp.load(lambda e: e.dma_start(wo_f[:, :, :], wo_d[p]), l_wo, wo_stage)
            wo_stage = split(at(wo, slice(None)), wo_f[:, :, :], t, free, lo=pool)
            return wo_stage

        t_wqk = [None] * NH
        t_pj = [None] * NH
        t_qk = [None] * NH
        t_sc = [None] * NH
        t_x = []
        for j in range(4):
            t_x.append(sp.load(lambda e, j=j: e.dma_start(xa[:, j, :], x_d[j]), l_x[j]))
            if j == 0:
                t_id = sp.load(lambda e: e.dma_start(ident[:, :], ident_d), l_c)
        t_xT = [None] * NA
        t_rs = {}

        t_zt = pool(lambda e: e.memset(zt[:, :], 0.0))
        for j in range(4, NA):
            t_x.append(sp.load(lambda e, j=j: e.dma_start(xa[:, j, :], x_d[j]), l_x[j]))
        ln = {}
        t_st = {}
        early = {}

        def project_qk_pe(h, n, j):
            w, i = wqk[h % 2], pj_next()
            for k in range(KC):
                t = mm3(PJ[i][:, 0:HT], at(w, slice(None), k, slice(j * 128, j * 128 + 128)),
                        at(xT, slice(None), k, slice(n * HT, n * HT + HT)), k == 0, k == KC - 1,
                        t_wqk[h], t_xT[3 * n + 3], pj_free[i], inc=k == KC - 1)
            return i, t

        for j in range(NA + 2):
            if j < NA:
                t = dve(lambda e, j=j: e.bn_stats(st[:, j, :], xa[:, j, :]), t_x[j])

                def aggregate(j=j, t=t):
                    t_st[j] = dve(lambda e: e.bn_aggr(mv[:, j, :], st[:, j, :]), t)
            if 1 <= j <= NA:
                i = j - 1
                ln[i] = ln_scale(xa[:, i, :], i, 128, t_rs[i], (aggregate,) if j < NA else ())
            elif j < NA:
                aggregate()
            if j < NA:
                t_rs[j] = rsqrt_start(j, 128, t_st[j])
            if 1 <= j <= NA:
                i = j - 1
                ln[i] = ln_turn(*ln[i], 128, TB[i % 2], tb_free[i % 2], None, 128 * i)
            if j >= 2:
                i = j - 2
                tb_free[i % 2] = t_xT[i] = ln_rest(*ln.pop(i))
            if j == 2:
                t_wqk[0] = prep_wqk(0, None)
            if j in (5, 6):
                early[0, 0, j - 5] = project_qk_pe(0, 0, j - 5)
        t_wvp = prep_wv(0, None)
        t_mask = sp.load(lambda e: e.dma_start(mask[:, :], mask_d), l_m)
        t_wqk[1] = prep_wqk(1, None)
        t_wop = prep_wo(0, None)

        def project_qk(h):
            t_done = []
            for n in range(2):
                for j in range(2):
                    i, t = early.pop((h, n, j), None) or project_qk_pe(h, n, j)
                    f = copy_act if j else copy_dve
                    pj_free[i] = f(qk[h % 2][:, j, n * HT:n * HT + HT], PJ[i][:, 0:HT], t, t_sc[h - 2] if h >= 2 else None)
                    t_done.append(pj_free[i])
            t_pj[h] = t
            t_qk[h] = t_done

        t_av = [None] * NH
        t_v = [None] * (NH // 2)

        def project_v(p):
            t_done = []
            for b in range(0, NB, 2):
                i = pj_next()
                for c in range(2):
                    for k in range(KC):
                        t = mm3(PJ[i][0:T, c * 256:c * 256 + 256],
                                at(xT, slice(None), k, slice((b + c) * T, (b + c + 1) * T)),
                                at(wv, slice(None), k, slice(None)), k == 0, k == KC - 1,
                                t_wvp, t_xT, pj_free[i], inc=k == KC - 1)
                f = copy_act if b % 4 else copy_dve
                pj_free[i] = f(vv[p % 2][:, b:b + 2, :], PJ[i][0:T, :].rearrange("p (c n) -> p c n", c=2), t,
                               t_av[2 * p - 3] if p >= 2 else None)
                t_done.append(pj_free[i])
            t_v[p] = t_done
            return t

        t_sm = [None, None]
        t_pn = [None, None]
        t_pt_pe = [None, None]

        def scores(h):
            q = qk[h % 2]
            for g in range(2):
                for c in range(4):
                    b = 4 * g + c
                    t = mm(SB_[g][0:T, c * T:(c + 1) * T], q[:, 0, b * T:(b + 1) * T], q[:, 1, b * T:(b + 1) * T],
                           True, True, t_qk[h], s_free[g], inc=c == 3)
                t_sc[h] = t
                t = tt(dve, sm[g][:, :, :], SB_[g][0:T, 0:4 * T].rearrange("p (c t) -> p c t", c=4),
                       mask[:, :].unsqueeze(1).to_broadcast([T, 4, T]), ALU.add, t, t_mask, t_sm[g])
                s_free[g] = t
                t = dve(lambda e, g=g: e.tensor_reduce(nm[g][:, :], sm[g][:, :, :], X, ALU.max, negate=True), t)
                t = dve(lambda e, g=g: e.tensor_scalar(nm[g][:, :], nm[g][:, :], ISQ, None, ALU.mult), t)
                for c in range(4):
                    t_sm[g] = act(lambda e, g=g, c=c: e.activation(
                        pp[g][:, c, :], sm[g][:, c, :], ACT.Exp, bias=nm[g][:, c:c + 1], scale=ISQ,
                        accum_out=rs[g][:, c:c + 1]), t, t_pt_pe[g])

        def normalise(h):
            for g in range(2):
                t = dve(lambda e, g=g: e.reciprocal(rc[g][:, :], rs[g][:, :]), t_sm[g])
                t_pn[g] = tt(dve, pp[g][:, :, :], pp[g][:, :, :],
                             rc[g][:, :].unsqueeze(2).to_broadcast([T, 4, T]), ALU.mult, t)

        t_pt = [None, None]

        def transpose_p(h):
            for g in range(2):
                for c in range(4):
                    t = tr(TB[g][0:T, c * T:(c + 1) * T], pp[g][:, c, :], ident[0:T, 0:T], t_pn[g], tb_free[g],
                           inc=c == 3)
                t_pt_pe[g] = t
                f = copy_act if g else copy_dve
                tb_free[g] = t_pt[g] = f(pt[g][:, :], TB[g][0:T, 0:4 * T], t, t_av[h - 1] if h else None)

        t_wo_pe = None
        t_z = None

        def weighted_v(h):
            nonlocal t_z
            o = (h % 2) * 128
            t_done = [t_z]
            for g in range(2):
                i = pj_next()
                for c in range(4):
                    t = mm(PJ[i][:, c * T:(c + 1) * T], vv[h // 2 % 2][:, 4 * g + c, o:o + 128],
                           pt[g][:, c * T:(c + 1) * T], True, True, t_pt[g], t_v[h // 2], pj_free[i], inc=c == 3)
                pj_free[i] = split(at(zT, slice(None), h % 2, slice(g * HT, g * HT + HT)), PJ[i][:, 0:HT], t, t_wo_pe)
            t_av[h] = t
            t_z = pj_free[i]

        t_res = list(t_x)
        l_r = [lane(f"r{b}") for b in range(NB)]
        t_rows = [None] * NB
        t_n2 = {}

        def batch_rows(b):
            r = 0
            while r < T:
                j, p = (b * T + r) // 128, (b * T + r) % 128
                n = min(T - r, 128 - p)
                t = sp.load(lambda e, r=r, j=j, p=p, n=n: e.dma_start(xs[r:r + n, b, :], xa[p:p + n, j, :]),
                            l_r[b], t_res[j])
                r += n
            t_rows[b] = t

        def project_o(p, tiles=range(NA)):
            nonlocal t_wo_pe
            for j in tiles:
                i = pj_next()
                for c in range(2):
                    t = mm3(PJ[i][:, :], at(zT, slice(None), c, slice(j * 128, (j + 1) * 128)),
                            at(wo, slice(None), c, slice(None)), c == 0, c == 1, t_z, t_wop, pj_free[i], inc=c == 1)
                pj_free[i] = t_res[j] = tt(dve, xa[:, j, :], xa[:, j, :], PJ[i][:, :], ALU.add, t, t_res[j])
            t_wo_pe = t

        t_wkv = []

        def prep_wkv(k, stage):
            t = sp.load(lambda e: e.dma_start(wv_f[:, :, :].rearrange("p a n -> p (a n)"),
                                              wkv_d[:, k * 1024:(k + 1) * 1024]), l_wx, stage)
            t_wkv.append(split(at(wkv, slice(None), k), wv_f[:, :, :].rearrange("p (a b) n -> p a (b n)", a=2),
                               t, lo=pool))

        l_cx = [lane("cx0"), lane("cx1")]
        t_ctx = {}

        project_qk(0)
        t_vpe = project_v(0)
        scores(0)
        normalise(0)

        ctx_stage = [None, None]
        ctx_use = [None] * 4

        def ctx_load(b, m):
            n = b * MC + m
            i = n % 2
            if b < NB:
                t_ctx[b, m] = sp.load(lambda e: e.dma_start(ctx_f[i][:, :, :], ctx_d[b, m]), l_cx[i], ctx_stage[i])

        def ctx_split(b, m):
            n = b * MC + m
            i, j = n % 2, n % 4
            if b < NB:
                ctx_stage[i] = t_ctx[b, m] = split(at(ctx[j], slice(None)), ctx_f[i][:, :, :], t_ctx[b, m], ctx_use[j],
                                                   lo=pool)

        for h in range(NH - 1):
            project_qk(h + 1)
            if h + 2 < NH:
                t_wqk[h + 2] = prep_wqk(h + 2, t_pj[h])
            if h % 2 == 0 and h + 2 < NH:
                t_wvp = prep_wv(h // 2 + 1, t_vpe)
            if h == 4:
                t_clear = sp.load(lambda e: e.dma_start(
                    slots_d.rearrange("(p r) (c d) -> p (r c) d", p=128, d=128),
                    zt[:, :].unsqueeze(1).to_broadcast([128, NBLK * BS // 32, 128])), l_z, t_zt)
            if h >= 13:
                prep_wkv(3 * h - 39, t_wkv[-1] if t_wkv else wv_stage)
            transpose_p(h)
            if h == NH - 2:
                for m in range(2):
                    ctx_split(0, m)
            scores(h + 1)
            weighted_v(h)
            normalise(h + 1)
            if h == NH - 3:
                prep_wkv(1, t_wkv[-1])
            if h == NH - 2:
                t_wqx = split([w[:, :, :] for w in wqx], wqx_f[:, :, :], t_wqx, t_pj[NH - 1])
                ctx_load(0, 2)
                ctx_load(1, 0)
            if h % 2:
                t_vpe = project_v(h // 2 + 1)
                project_o(h // 2)
                t_wop = prep_wo(h // 2 + 1, t_wo_pe)
            if h == NH - 3:
                t_wqx = sp.load(lambda e: e.dma_start(wqx_f[:, :, :].rearrange("p a n -> p (a n)"), wqx_d), l_wq, wqk_stage)
                prep_wkv(2, t_wkv[-1])
                ctx_stage = [wo_stage] * 2
                ctx_load(0, 0)
                ctx_load(0, 1)

        done_e, done_a = [], []

        NU = 2 * NB
        room = {
            "xa": [base, base + NA * D * 4], "mask": [base + NA * D * 4, place_f], "wqx_f": [place_f, place_w],
            "wv": [place_w + 2 * KC * D * 4, place_wo], "wo": [place_w2, place_qk], "mid": [place_qk, place_z],
            "z": [place_z, place_z2], "end": [place_z2, end_a], "free": [start_p, top - 32768],
        }

        def sbl(name, shape, dt, where):
            n = 4
            for s in shape[1:]:
                n *= s
            t = nc.alloc_sbuf_tensor_at(name, shape, dt, offset=room[where][0])
            room[where][0] += n + 31 & ~31
            assert room[where][0] <= room[where][1], (name, room)
            return t

        def pairl(name, shape, where):
            return sbl(name + "_hi", shape, F32R, where), sbl(name + "_lo", shape, F32R, where)

        kT = [sbl(f"kT{i}", [128, 8, M], F32R, "mid") for i in range(2)]
        vb = [sbl(f"vb{i}", [MS, MC, XH, VW], F32R, "mid") for i in range(2)]
        qT = [sbl(f"qT{i}", [128, 8, 2, T], F32R, "z") for i in range(2)]
        kk = [sbl(f"kk{i}", [MS, XH, 4, 16], F32R, "wv") for i in range(2)]
        ctx += [pairl(f"ctx{i}", [128, KC, MS], "wqx_f") for i in (2, 3)]
        ep = [pairl(f"ep{i}", [MS, 4 * T], "xa" if i < 4 else "wo") for i in range(6)]
        ee = [sbl(f"ee{i}", [MS, 4 * T], F32, w) for i, w in enumerate(("wv", "wv", "mid"))]
        oo = [sbl(f"oo{i}", [VW, 4 * T], F32, w) for i, w in enumerate(("mid", "mask"))]
        kn = sbl("kn", [MS, 256], F32, "free")
        ss = [sbl(f"ss{i}", [MS, XH], F32, "mid") for i in range(2)]
        rr = [sbl(f"rr{i}", [MS, XH], F32, "mid") for i in range(2)]
        rq = [sbl(f"rq{i}", [MS, XH], F32, "mid") for i in range(2)]
        zz = sbl("zz", [T, 4, 16], F32, "wv")
        zc = sbl("zc", [T, 4], F32, "wv")
        gw_f = sbl("gw_f", [128, KC, NE], F32, "wv")
        gw = pairl("gw", [128, KC, NE], "mid")
        lT = [sbl(f"lT{i}", [NE, T], F32, w) for i, w in enumerate(("wo", "mask"))]
        lg = sbl("lg", [T, NB, NE], F32, "mask")

        t_one = None
        t_zero = []

        KB, SX, AB, TX = banks[0:2], banks[2:5], banks[5], banks[6:8]
        kb_free, sx_free, tx_free = pj_free[0:2], [pj_free[2], pj_free[3], s_free[0]], list(tb_free)
        ab_free = s_free[1]
        n_kb, n_sx, n_tx, n_ep = [0], [0], [0], [0]

        def turn(c, n):
            i = c[0] % n
            c[0] += 1
            return i

        vb_free, kT_free, qT_free = [done_e] * 2, [done_e] * 2, [done_a] * 2
        kn_free, kk_free = done_e, [done_e] * 2
        t_kT, t_qT, t_vb = [None] * NU, [None] * NU, [None] * NU
        rows = {}
        n_row = [0]

        kx = "q"

        def rows_pe(u, m):
            b, hf = u // 2, u % 2
            i, r = turn(n_kb, 2), turn(n_row, 2)
            if m == kx:
                for k in range(KC):
                    t = mm3(KB[i][0:T, 0:256], at(xT, slice(None), k, slice(b * T, (b + 1) * T)),
                            at(wqx, slice(None), k, slice(hf * 256, hf * 256 + 256)), k == 0, k == KC - 1,
                            t_xT2[b], t_wqx, kb_free[i], inc=k == KC - 1)
                t_q_pe[b] = t
                rows[u, m] = [i, r, T, t]
            else:
                j = (b * MC + m) % 4
                for k in range(KC):
                    t = mm3(KB[i][0:MS, :], at(ctx[j], slice(None), k, slice(None)),
                            at(wkv, slice(None), k, hf, slice(None)), k == 0, k == KC - 1,
                            t_ctx[b, m], t_wkv, kb_free[i], inc=k == KC - 1)
                ctx_use[j] = t
                rows[u, m] = [i, r, MS, t]

        def rows_square(u, m):
            i, r, R, t = rows[u, m]
            src, to = KB[i][0:R, 0:256], kk[r][0:R, :, 0, :].bitcast(F32)
            t_s = act(lambda e: e.activation(to, src.rearrange("p (h d) -> p h d", d=16), ACT.Square), t, kk_free[r])
            t_v = t_s
            if m != kx:
                t_v = copy_act(vb[u % 2][:, m, :, 0:16], KB[i][0:MS, 256:512].rearrange("p (h d) -> p h d", d=16), t,
                               vb_free[u % 2], t_one)
            rows[u, m] += [t_s, t_v]

        def rows_sum(u, m):
            i, r, R, t, t_s, t_v = rows[u, m]
            t = dve(lambda e: e.tensor_reduce(ss[r][0:R, :], kk[r][0:R, :, 0, :].bitcast(F32), X, ALU.add), t_s)
            rows[u, m][3] = t
            if m != kx:
                vh, vl = vb[u % 2][:, m, :, 0:16], vb[u % 2][:, m, :, 16:32]
                t_vb[u] = tt(dve, vl, KB[i][0:MS, 256:512].rearrange("p (h d) -> p h d", d=16), vh.bitcast(F32),
                             ALU.subtract, t_v, vb_free[u % 2])

        def rows_root(u, m):
            i, r, R, t = rows[u, m][0:4]
            t = act(lambda e: e.activation(rr[r][0:R, :], ss[r][0:R, :], ACT.Ln, scale=1.0 / 16, bias=epsc[0:R, 0:1]),
                    t, t_eps)
            rows[u, m][3] = act(lambda e: e.activation(rr[r][0:R, :], rr[r][0:R, :], ACT.Exp, scale=-0.5), t)

        def rows_finish(u, m, between=()):
            nonlocal kn_free
            i, r, R, t, t_s, t_v = rows[u, m]
            y, tmp, v = rr[r][0:R, :], rq[r][0:R, :], ss[r][0:R, :]
            t = dve(lambda e: e.scalar_tensor_tensor(tmp, y, -1.0 / 32, y, ALU.mult, ALU.mult), t)
            for go in between[:1]:
                go()
            t = dve(lambda e: e.scalar_tensor_tensor(tmp, v, 16e-6, tmp, ALU.add, ALU.mult), t)
            for go in between[1:]:
                go()
            t = dve(lambda e: e.scalar_tensor_tensor(y, tmp, 1.5, y, ALU.add, ALU.mult), t)
            t = tt(dve, kn[0:R, :].rearrange("p (h d) -> p h d", d=16),
                   KB[i][0:R, 0:256].rearrange("p (h d) -> p h d", d=16),
                   rr[r][0:R, :].unsqueeze(2).to_broadcast([R, XH, 16]), ALU.mult, t, t_s, t_v, kn_free)
            kb_free[i] = t
            row = kn[0:R, :].rearrange("p (h d) -> p h d", d=16)
            twice = row.unsqueeze(2).to_broadcast([R, XH, 2, 16])
            o = kk[r][0:R, :, :, :]
            if m == kx:
                hi, lo, first = o[:, :, 0:2, :], o[:, :, 2:4, :], o[:, :, 0, :]
            else:
                o = o.rearrange("p h (a c) d -> p h a c d", c=2)
                hi, lo, first = o[:, :, :, 0, :], o[:, :, :, 1, :], kk[r][0:R, :, 0, :]
            t = copy_dve(hi, twice, t, kk_free[r])
            first2 = first.bitcast(F32).unsqueeze(2).to_broadcast([R, XH, 2, 16])
            kn_free = rows[u, m][3] = tt(pool, lo, twice, first2, ALU.subtract, t)

        def rows_turn(u, m):
            i, r, R, t = rows[u, m][0:4]
            turned = []
            s = kk[r][0:R, :, :, :].bitcast(F32).rearrange("p (g h) a d -> p g (h a d)", h=2)
            for c in range(2):
                i = turn(n_tx, 2)
                for g in range(4):
                    tp = tr(TX[i][:, g * R:(g + 1) * R], s[:, 4 * c + g, :], ident[0:R, 0:R], t, tx_free[i], inc=g == 3)
                turned.append((i, tp))
            kk_free[r] = tp
            rows[u, m] = turned, R

        def rows_copy(u, m):
            turned, R = rows.pop((u, m))
            for c, (i, tp) in enumerate(turned):
                src = TX[i][:, 0:4 * R].rearrange("p (g t) -> p g t", g=4)
                if m == kx:
                    tx_free[i] = [q(qT[u % 2][64 * o:64 * o + 64, 4 * c:4 * c + 4, o, :], src[64 * o:64 * o + 64],
                                    tp, qT_free[u % 2], t_zero) for o, q in enumerate((copy_act, copy_dve))]
                    t_qT[u] = tx_free[i]
                else:
                    tx_free[i] = copy_act(kT[u % 2][:, 4 * c:4 * c + 4, m * MS:(m + 1) * MS], src, tp, kT_free[u % 2])
                    t_kT[u] = tx_free[i]

        ee_free, ep_free = [done_a] * 3, [[done_a, t_rows]] * 6
        oo_free = [done_a] * 2
        probs = {}
        outs = {}
        n_ee = [0]
        n_oo = [0]
        LO_POOL = (1, 2)

        def score_pe(u, q):
            for m in range(MC):
                i = turn(n_sx, 3)
                for c in range(2):
                    t = mm(SX[i][0:MS, c * 2 * T:(c + 1) * 2 * T], kT[u % 2][:, 2 * q + c, m * MS:(m + 1) * MS],
                           qT[u % 2][:, 2 * q + c, :, :], True, True, t_kT[u], t_qT[u], sx_free[i], inc=c == 1)
                if m == MC - 1 and q == 3:
                    kT_free[u % 2] = qT_free[u % 2] = t
                e = turn(n_ee, 3)
                t = act(lambda en, e=e, i=i: en.activation(ee[e][:, :], SX[i][0:MS, 0:4 * T], ACT.Exp, scale=0.25),
                        t, ee_free[e])
                sx_free[i] = t
                probs[u, q, m] = (e, t)

        def score_split(u, q):
            for m in range(MC):
                e, t = probs[u, q, m]
                p = turn(n_ep, 6)
                t = copy_dve(ep[p][0][:, :], ee[e][:, :], t, ep_free[p])
                t = tt(pool if m in LO_POOL else dve, ep[p][1][:, :], ee[e][:, :], ep[p][0][:, :].bitcast(F32),
                       ALU.subtract, t, ep_free[p])
                ee_free[e] = t
                probs[u, q, m] = (p, t)

        def value_pe(u, q):
            for c in range(4):
                for m in range(MC):
                    p, t = probs[u, q, m]
                    w = vb[u % 2][:, m, 4 * q + c, :]
                    o = AB[0:VW, c * T:(c + 1) * T]
                    mm(o, w, ep[p][0][:, c * T:(c + 1) * T], m == 0, False, t, t_vb[u], t_one, ab_free)
                    t = mm(o, w, ep[p][1][:, c * T:(c + 1) * T], False, m == MC - 1, inc=c == 3)
                    if c == 3:
                        ep_free[p] = t
            if q == 3:
                vb_free[u % 2] = t
            outs[u, q] = t

        def value_copy(u, q):
            nonlocal ab_free
            i = turn(n_oo, 2)
            ab_free = copy_act(oo[i][:, :], AB[0:VW, 0:4 * T], outs[u, q], oo_free[i])
            outs[u, q] = (i, ab_free)

        t_zz = done_a
        t_row2 = t_rows

        def out_pe(u, q):
            i, t = outs.pop((u, q))
            j = turn(n_sx, 3)
            for c in range(4):
                tp = tr(SX[j][0:T, c * VW:(c + 1) * VW], oo[i][:, c * T:(c + 1) * T], ident[0:VW, 0:VW], t,
                        sx_free[j], inc=c == 3)
            oo_free[i] = tp
            outs[u, q] = (j, tp)

        def out_add(u, q):
            b, hf = u // 2, u % 2
            j, tp = outs.pop((u, q))
            o = SX[j][0:T, 0:4 * VW].rearrange("p (c w) -> p c w", w=VW)
            t0 = dve(lambda e: e.reciprocal(zc[:, :], o[:, :, 32]), tp, t_zz)
            t1 = dve(lambda e: e.tensor_reduce(zz[:, :, :], o[:, :, 0:32].rearrange("p c (a d) -> p c d a", a=2),
                                               X, ALU.add), tp, t_zz)
            sx_free[j] = t1
            n = (hf * XH + 4 * q) * 16
            row = xs[:, b, n:n + 64].rearrange("p (c d) -> p c d", d=16)
            t_mul = []

            def multiply():
                t_mul.append(tt(dve, zz[:, :, :], zz[:, :, :], zc[:, :].unsqueeze(2).to_broadcast([T, 4, 16]),
                                ALU.mult, t0, t1))

            def add():
                nonlocal t_zz
                t_zz = t_row2[b] = tt(dve, row, row, zz[:, :, :], ALU.add, t_mul[0], t_row2[b], t_ln[b])

            to_add[:] = multiply, add

        to_add = []

        t_ln = [None] * NB
        t_xT2, t_xT3 = [None] * NB, [None] * NB
        t_q_pe = [None] * NB
        t_lT, t_lg = [done_a] * 2, [None] * NB
        t_n3 = {}

        def second_norm(b, part):
            if part == 0:
                t_n2[b] = ln_stats(xs[:, b, :], b, T, t_rows[b], t_xa)
            elif part == 1:
                t_n2[b] = rsqrt_start(b, T, t_n2[b])
            elif part == 2:
                t_n2[b] = ln_scale(xs[:, b, :], b, T, t_n2[b])
                t_ln[b] = t_n2[b][1]
            elif part == 3:
                j = turn(n_tx, 2)
                t_n2[b] = (j,) + ln_turn(*t_n2[b], T, TX[j], tx_free[j], done_a, b * T)
            else:
                j, *rest = t_n2[b]
                tx_free[j] = t_xT2[b] = ln_rest(*rest)

        def third_norm(b, part):
            if part == 0:
                t_n3[b] = ln_stats(xs[:, b, :], b, T, t_row2[b])
            elif part == 1:
                t_n3[b] = rsqrt_start(b, T, t_n3[b])
            elif part == 2:
                t_n3[b] = ln_scale(xs[:, b, :], b, T, t_n3[b])
            elif part == 3:
                j = turn(n_tx, 2)
                t_n3[b] = (j,) + ln_turn(*t_n3[b], T, TX[j], tx_free[j], t_q_pe[b], b * T)
            else:
                j, *rest = t_n3[b]
                tx_free[j] = t_xT3[b] = ln_rest(*rest)

        def gate(b, part):
            i = b % 2
            j = turn(n_tx, 2)
            if part == 5:
                for k in range(KC):
                    t = mm3(TX[j][0:NE, 0:T], at(gw, slice(None), k, slice(None)),
                            at(xT, slice(None), k, slice(b * T, (b + 1) * T)), k == 0, k == KC - 1,
                            t_xT3[b], t_gw, tx_free[j], inc=k == KC - 1)
                tx_free[j] = t_lg[b] = copy_act(lT[i][:, :], TX[j][0:NE, 0:T], t, t_lT[i])
            else:
                t = t_lT[i] = tr(TX[j][0:T, 0:NE], lT[i][:, :], ident[0:NE, 0:NE], t_lg[b], tx_free[j], inc=True)
                tx_free[j] = t_lg[b] = copy_dve(lg[:, b, :], TX[j][0:T, 0:NE], t, done_a)

        ahead = [(0, 0), (0, 1)]

        def step(new, mid, old, quad, nxt, prev, norm, first):
            def project():
                if new and new not in ahead:
                    rows_pe(*new)

            boundary = nxt and nxt[1] == 0
            if first:
                project()
            if mid:
                rows_sum(*mid)
                rows_root(*mid)
            if mid and first:
                rows_finish(*mid)
            if old:
                rows_turn(*old)
                if first or boundary:
                    rows_copy(*old)
            if norm and norm[2] == 1:
                norm[0](*norm[1:])
            if boundary and not first:
                project()
            if nxt:
                score_pe(*nxt)
            if old and not first and not boundary:
                rows_copy(*old)
            if mid and not first:
                rows_finish(*mid, between=to_add)
            else:
                for go in to_add:
                    go()
            del to_add[:]
            if nxt:
                score_split(*nxt)
            if not boundary and not first:
                project()
            if norm and norm[2] == 3:
                norm[0](*norm[1:])
                norm[0](norm[1], 4)
            if boundary and quad:
                value_pe(*quad)
            if prev:
                out_pe(*prev)
                out_add(*prev)
            if norm and norm[2] in (0, 1):
                norm[0](norm[1], 2 * norm[2])
            if norm and norm[2] > 4:
                norm[0](*norm[1:])
            if quad and not boundary:
                value_pe(*quad)
            if new:
                rows_square(*new)
                u, m = new
                if u % 2:
                    nb, nm = (u // 2 + 1, m + 1) if m in (0, 1) else (u // 2 + 2, 0) if m == 2 else (NB, 0)
                    ctx_load(nb, nm)
                    ctx_split(nb, nm)
            if quad:
                value_copy(*quad)

        t_xa = t_xT[NA - 1]
        items = [(0, 0), (0, 1), (0, 2), (0, kx)]
        items += [(u, m) for u in range(1, NU) for m in (kx, 0, 1, 2)] + [None] * 8
        quads = [(u, q) for u in range(NU) for q in range(4)] + [None]
        norms = {}
        for b in range(NB):
            for i, part in enumerate((0, 1, 3)):
                norms[8 * b - 1 + i] = (second_norm, b + 1, part) if b + 1 < NB else None
                norms[8 * b + 10 + i] = (third_norm, b, part)
            norms[8 * b + 13] = (gate, b, 5)
            norms[8 * b + 14] = (gate, b, 6)
        def over(name, shape, dt, offset):
            n = 4
            for d in shape[1:]:
                n *= d
            assert offset % 32 == 0 and offset + n <= top, (name, offset, n, top)
            return nc.alloc_sbuf_tensor_at(name, shape, dt, offset=offset)

        SC = KC * 256 + D
        o = top - 32768
        F = [None, over("F1", [128, WE], F32, o)]
        sf = [[over(f"sf{i}", [128, SC], F32, o + i * SC * 4) for i in range(2)]]
        o += WE * 4
        S0 = [over(f"S0{n}", [128, SC], F32R, o + i * SC * 4) for i, n in enumerate(("hi", "lo"))]
        S1 = [over(f"S1{n}", [128, SC], F32R, place_w + i * SC * 4) for i, n in enumerate(("hi", "lo"))]
        assert o + 2 * SC * 4 <= top and SC <= KC * D
        sg, hh, hs = [], [], []
        o = end_a
        for x_ in (sg, hh):
            x_.append(over(f"sg{o}", [128, HT], F32, o))
            o += HT * 4
        hs.append([over(f"hs0{n}", [128, HT], F32R, o + i * HT * 4) for i, n in enumerate(("hi", "lo"))])
        assert o + 2 * HT * 4 <= start_p
        hT = [over("hT0", [128, 3, BS], F32R, o)]
        o = place_w + 2 * SC * 4
        S2 = [over("S2hi", [128, SC], F32R, place_f), over("S2lo", [128, SC], F32R, o)]
        sg.append(over("sg_s", [128, HT], F32, place_f + SC * 4))
        o += SC * 4
        hh.append(over("hh_s", [128, HT], F32, o))
        hs.append([over(f"hs_s{n}", [128, HT], F32R, o + (i + 1) * HT * 4) for i, n in enumerate(("hi", "lo"))])
        end_s = o + 3 * HT * 4
        assert SC * 4 + HT * 4 <= place_w - place_f and end_s <= place_w + 2 * KC * D * 4 + 2 * XH * 64 * 4
        ring = [[S0, S1, S2], [S0]]
        l_sf = [lane("sf0"), lane("sf1")]
        sf_free, slot_free = [None, None], [None, None, None]
        t_sf, t_we = {}, {}

        def chunk_load(n, c, o=0):
            i = c % 2
            t_sf[n, c] = sp.load(lambda e: e.dma_start(sf[n][i][:, o:], moe_d[c, :, o:]), l_sf[i], sf_free[i])

        def chunk_split(n, c, m, o=0):
            i, j = c % 2, c % 3
            w = ring[n][j]
            t = copy_act(w[0][:, o:], sf[n][i][:, o:], t_sf[n, c], slot_free[j])
            sf_free[i] = t_we[n, c] = [
                tt(q, w[1][:, z], sf[n][i][:, z], w[0][:, z].bitcast(F32), ALU.subtract, t)
                for q, z in ((dve, slice(max(m, o), SC)), (pool, slice(o, m))) if z.start < z.stop]

        GU, AC = [banks[0], banks[1], banks[6], banks[7]], banks[2:6]
        gu_free, ac_free = [None] * 4, [None] * 4
        n_gu = [0]

        t_hs = {}
        hs_free, sg_free, hh_free = [None] * 2, [None] * 2, [None] * 2
        t_up = {}

        def up_pe(n, c, parts=(0, 1), early=False):
            w, t_w = ring[0 if early else n][c % 3], t_we[0 if early else n, c]
            for a in parts:
                g = turn(n_gu, 4)
                for k in range(KC):
                    o = k * 256 + a * 128
                    t = mm3(GU[g][:, 0:HT], at(w, slice(None), slice(o, o + 128)),
                            at(xT, slice(None), k, slice(n * HT, n * HT + HT)), k == 0, k == KC - 1,
                            t_w, t_xT3[4 * n:4 * n + 4], gu_free[g], inc=k == KC - 1)
                t_up[n, c, a] = (g, t)

        def up_act(n, c, later=False):
            (g, tg), (u, tu) = t_up.pop((n, c, 0)), t_up.pop((n, c, 1))
            j = c % 2
            s_ = sg[j][:, :]
            t = act(lambda e: e.activation(s_, GU[g][:, 0:HT], ACT.Silu), tg, sg_free[j])
            gu_free[g] = t
            t = tt(dve, hh[j][:, :], s_, GU[u][:, 0:HT], ALU.mult, t, tu, hh_free[j])
            gu_free[u] = sg_free[j] = t
            hi, lo, h_ = hs[j][0][:, :], hs[j][1][:, :], hh[j][:, :]
            t = copy_act(hi, h_, t, hs_free[j])

            def low():
                hh_free[j] = t_hs[n, c] = tt(dve, lo, h_, hi.bitcast(F32), ALU.subtract, t, hs_free[j])
            if later:
                return low
            low()

        LAST = (NS - 1, NS - 2)

        def down(n, c, tiles=range(4), h=None):
            w = ring[n][c % 3]
            j = c % 2
            h = h or hs[j]
            for b in tiles:
                t = mm3(AC[b][0:T, :], at(h, slice(None), slice(b * T, (b + 1) * T)),
                        at(w, slice(None), slice(1024, 1536)), c == 0, c == LAST[n], t_we[n, c], t_hs[n, c], ac_free[b], inc=True)
                if c == LAST[n]:
                    t_ac[4 * n + b] = t
            hs_free[j] = slot_free[c % 3] = t

        t_ac = [None] * NB

        LEAD = 6

        def run(s):
            n = s + LEAD
            step(items[n], items[n - 1] if n else None, items[n - 2] if n > 1 else None, quads[s] if s >= 0 else None,
                 quads[s + 1] if s >= -1 else None, quads[s - 1] if s >= 1 else None, norms.get(s), s < 0)

        h = NH - 1
        rows_pe(0, 0)
        rows_pe(0, 1)
        pj_use[:] = [2, 3, 4, 5]
        pj_free[4:6] = s_free
        transpose_p(h)
        ctx_use[2:4] = [t_wqx] * 2
        ctx_split(0, 2)
        weighted_v(h)
        ctx_split(1, 0)
        tx_free[:] = tb_free
        done_e += [q.last() for q in (pe, act, dve, pool)]
        t_eps = pool(lambda e: e.memset(epsc[:, 0:1], 1e-6), done_e)
        for i in range(2):
            pool(lambda e, i=i: e.memset(vb[i][:, :, :, 32:33].bitcast(F32), 1.0), done_e)
            t_one = pool(lambda e, i=i: e.memset(vb[i][:, :, :, 33:34].bitcast(F32), 0.0), done_e)
        xn_use[0] = 1

        def last_rows(*tiles):
            project_o(h // 2, tiles)
            for b in range(NB):
                if ((b + 1) * T - 1) // 128 in tiles:
                    batch_rows(b)

        run(-6)
        last_rows(0, 1)
        run(-5)
        last_rows(2)
        t_n2[0] = ln_stats(xs[:, 0, :], 0, T, t_rows[0], t_xa)
        t_n2[0] = rsqrt_start(0, T, t_n2[0])
        last_rows(3)
        run(-4)
        second_norm(0, 2)
        last_rows(4)
        second_norm(0, 3)
        second_norm(0, 4)
        last_rows(5)
        run(-3)
        last_rows(6)
        done_a += [q.last() for q in (pe, act, dve, pool)]
        sx_free[:] = pj_free[2:5]
        ab_free = pj_free[5]
        t_zero += [pool(lambda e, i=i: e.memset(qT[i][:, :, :, :].bitcast(F32), 0.0), done_a) for i in range(2)]
        t_gw = sp.load(lambda e: e.dma_start(gw_f[:, :, :], gw_d), l_g, done_a)
        for s in range(-2, 4 * NU):
            if s == 4 * NU - 5:
                slot_free[:2] = sf_free[:] = [pe.last()] * 2
                hs_free[0] = sg_free[0] = hh_free[0] = pe.last()
                chunk_load(0, 0)
                chunk_load(0, 1)
            if s == 4 * NU - 4:
                slot_free[2] = hs_free[1] = sg_free[1] = hh_free[1] = pe.last()
            if s >= 4 * NU - 4 and s < 4 * NU - 1:
                c = s - 4 * NU + 4
                chunk_split(0, c, 1024)
                chunk_load(0, c + 2)
            run(s)
            if s == 0:
                t_gw = split(at(gw, slice(None)), gw_f[:, :, :], t_gw, done_a, lo=pool)
            if s == 4 * NU - 3:
                gu_free[0:2] = kb_free
                up_pe(0, 0, (0,))
            if s == 4 * NU - 2:
                up_pe(0, 0, (1,))
                up_act(0, 0)
                exp_table()
                gu_free[2:4] = tx_free
            if s == 4 * NU - 1:
                up_pe(0, 1, (0,))

        place[0] = base
        xg = [sb(f"xg{i}", [128, 2, D], F32) for i in range(2)]
        xgT = pair("xgT", [128, KC, BS])
        E, EW = [None, None], [None, None]
        for i in (1, 0):
            EW[i] = place[0]
            E[i] = pair(f"E{i}", [128, WE])
        sf.append([over(f"sf_2{i}", [128, SC], F32, place[0] + i * SC * 4) for i in range(2)])
        F[0] = sb("F0", [128, WE], F32)
        assert 2 * SC <= WE
        assert EW[1] <= place_f and end_s <= EW[0]
        for k in range(2):
            ring[1].append([over(f"S{k + 3}{n}", [128, SC], F32R, EW[0] + (2 * k + i) * SC * 4)
                            for i, n in enumerate(("hi", "lo"))])
        sg1, hh1 = sb("sg1", [128, HT], F32), sb("hh1", [128, HT], F32)
        hT.append(over("hT1", [128, 3, BS], F32R, place[0]))
        hs1 = pair("hs1", [128, HT])
        yg = [sb(f"yg{i}", [128, D], F32) for i in range(4)]
        place_t = place[0]
        tab = sb("tab", [T, 2 * T + NE * NE + NBLK * NE], F32)
        small, o = {}, start_p
        for n, w in (("pr", 64), ("p2", 64), ("eq", 64), ("oh0", 64), ("oh1", 64), ("oc", 64), ("sc", 64),
                     ("le", NBLK * NE), ("cum", 72), ("mx", 8), ("m1", 8), ("m2", 8), ("f", 8), ("n", 8), ("cb", 8),
                     ("fs", 16)):
            if n in ("pr", "p2", "eq", "oh0", "mx", "m1", "m2", "f", "n", "cb"):
                small[n] = over("t_" + n, [T, w], F32, o)
                o += 4 * w
            else:
                small[n] = sb("t_" + n, [T, w], F32)
        assert o <= top - 32768, (o, start_p, top - 32768, place[0], end_a)
        assert place[0] <= end_a, (place[0], end_a)
        l_F = [lane("F0"), lane("F1")]
        l_xg = [lane("xg0"), lane("xg1")]
        l_yg, l_yo = [lane(f"yg{i}") for i in range(8)], [lane(f"yo{i}") for i in range(4)]
        l_out, l_tab = lane("out"), lane("tab")

        out_pe(NU - 1, 3)
        for go in to_add:
            go()
        out_add(NU - 1, 3)
        for go in to_add:
            go()
        TX[:] = banks[3:5]
        tx_free[:] = sx_free[1:3]
        third_norm(NB - 1, 0)
        third_norm(NB - 1, 1)
        third_norm(NB - 1, 2)
        up_pe(0, 1, (1,))
        up_pe(0, 2, (0,))
        third_norm(NB - 1, 3)
        third_norm(NB - 1, 4)
        ac_free[0], ac_free[3] = sx_free[0], ab_free
        down(0, 0, (0,))
        gate(NB - 1, 5)
        gate(NB - 1, 6)
        done_b = [q.last() for q in (pe, act, dve, pool)]
        up_pe(0, 2, (1,))
        ac_free[1:3] = tx_free
        t_tab = sp.load(lambda e: e.dma_start(tab[:, 0:T], cst_d[:, 0:T]), l_tab, done_b)
        t_tab = sp.load(lambda e: e.dma_start(tab[:, 2 * T:], cst_d[:, T:]), l_tab, done_b)
        down(0, 0, (3, 1, 2))

        def m3(name):
            return small[name][:, 0:64].rearrange("p (b e) -> p b e", e=NE)

        def v(name):
            return small[name][:, 0:8]

        def each(ap):
            return ap.unsqueeze(2).to_broadcast([T, NB, NE])

        def reduce(out, in_, op, *needs):
            return dve(lambda e: e.tensor_reduce(out, in_, X, op), *needs)

        pr, p2, eq, oh, oc, sc = m3("pr"), m3("p2"), m3("eq"), [m3("oh0"), m3("oh1")], m3("oc"), m3("sc")
        o = 2 * T
        NC = -(-NT // BS)
        consts = st[0:T, :, :].rearrange("p b s -> p (b s)")
        for i in range(NE + NC):
            t_consts = pool(lambda e, i=i: e.memset(consts[:, i:i + 1], float(NE - i if i < NE else (i - NE) * BS)),
                            done_b)
        t_ones = pool(lambda e: e.memset(tab[:, T:2 * T], 1.0), done_b)
        t_c0 = pool(lambda e: e.memset(small["cum"][:, 0:NE], 0.0), done_b)
        rev = consts[:, 0:NE].unsqueeze(1).to_broadcast([T, NB, NE])
        below = tab[:, o:o + NE * NE].rearrange("p (e f) -> p e f", f=NE)
        numbers = tab[0:1, o + NE * NE:].rearrange("p (j e) -> p j e", e=NE)
        starts = consts[:, NE:NE + NC].unsqueeze(1).to_broadcast([T, NE, NC])
        t = reduce(v("mx"), lg[:, :, :], ALU.max, t_lg, done_b)
        t = tt(dve, pr, lg[:, :, :], each(v("mx")), ALU.subtract, t)
        t = act(lambda e: e.activation(pr, pr, ACT.Exp), t)
        t = reduce(v("mx"), pr, ALU.add, t)
        t = dve(lambda e: e.reciprocal(v("mx"), v("mx")), t)
        t_p = tt(dve, pr, pr, each(v("mx")), ALU.mult, t)

        yb = [yg[i][0:T, :] for i in range(4)] + [xg[i // 2][0:T, i % 2, :] for i in range(4)]
        t_rowsx = None

        def rows_normal(b):
            nonlocal t_rowsx
            t_rowsx = dve(lambda e: e.tensor_scalar(yb[b], xs[:, b, :], mv[0:T, b, 0:1], rstd[0:T, b:b + 1],
                                                    ALU.subtract, ALU.mult), done_b)

        def largest(src, m, k, t, between=()):
            t = t_m = reduce(m, src, ALU.max, t)
            for go in between[:1]:
                go()
            t = tt(dve, eq, src, each(m), ALU.is_equal, t)
            t = tt(dve, eq, eq, rev, ALU.mult, t, t_consts)
            for go in between[1:]:
                go()
            t = reduce(v("f"), eq, ALU.max, t)
            return t_m, tt(dve, oh[k], each(v("f")), rev, ALU.is_equal, t)

        t_m1, t0 = largest(pr, v("m1"), 0, t_p)
        low = [up_act(0, 1, later=True)]
        t = dve(lambda e: e.scalar_tensor_tensor(p2, oh[0], -2.0, pr, ALU.mult, ALU.add), t0)
        t_m2, t1 = largest(p2, v("m2"), 1, t, (low[0], lambda: low.append(up_act(0, 2, later=True))))
        chunk_split(0, 3, SC)
        chunk_load(0, 5)
        t_oc = t = tt(dve, oc, oh[0], oh[1], ALU.add, t0, t1)
        cum = small["cum"][:, :].rearrange("p (b e) -> p b e", e=NE)
        low[1]()
        src = oc
        for n, to in ((1, eq), (2, sc), (4, cum[:, 1:, :])):
            t = [tt(dve, to[:, n:, :], src[:, n:, :], src[:, 0:NB - n, :], ALU.add, t, t_c0),
                 copy_dve(to[:, 0:n, :], src[:, 0:n, :], t, t_c0)]
            src = to
        t_cum = t
        down(0, 1)
        R = turn(n_gu, 4)
        cnt = GU[R][0:T, 64:72]
        mm(GU[R][0:T, 0:64], tab[:, 0:T], small["oc"][:, :], True, False, t_oc, t_tab, gu_free[R])
        mm(GU[R][0:T, 0:64], tab[:, T:2 * T], small["cum"][:, 0:64], False, True, t_cum, t_ones)
        t_rank = mm(cnt, tab[:, T:2 * T], small["cum"][:, 64:72], True, True, inc=True)
        down(0, 2)
        up_pe(0, 3)
        rows_normal(0)
        t = dve(lambda e: e.scalar_tensor_tensor(v("f"), v("m1"), 1e-20, v("m2"), ALU.add, ALU.add), t_m1, t_m2, t1)
        t = dve(lambda e: e.reciprocal(v("f"), v("f")), t)
        ta = tt(dve, w01[:, 0, :], v("m1"), v("f"), ALU.mult, t)
        t_w01 = [ta, tt(dve, w01[:, 1, :], v("m2"), v("f"), ALU.mult, t)]
        more = small["sc"][:, 0:NE * NC].rearrange("p (e i) -> p e i", i=NC)
        t = tt(dve, more, cnt.unsqueeze(2).to_broadcast([T, NE, NC]), starts, ALU.is_gt, t_rank, t_consts)
        t = reduce(v("n"), more, ALU.add, t)
        t = tt(dve, sc, small["n"][:, 0:8].unsqueeze(1).to_broadcast([T, NE, NE]), below, ALU.mult, t, t_tab)
        t = reduce(v("cb"), sc, ALU.add, t)
        t_cb = t
        t = dve(lambda e: e.scalar_tensor_tensor(p2, small["cb"][:, 0:8].unsqueeze(1).to_broadcast([T, NB, NE]),
                                                 float(BS), GU[R][0:T, 0:64].rearrange("p (b e) -> p b e", e=NE),
                                                 ALU.mult, ALU.add), t)
        gu_free[R] = t
        t_slot = []
        for k in range(2):
            ts = tt(dve, sc if k else eq, oh[k], p2, ALU.mult, t)
            t_slot.append(reduce(small["fs"][:, 8 * k:8 * k + 8], sc if k else eq, ALU.add, ts))
        t_slot = copy_dve(slot[:, :, :], small["fs"][:, :].rearrange("p (k b) -> p k b", k=2), t_slot)

        le = small["le"][0:1, :].rearrange("p (j e) -> p j e", e=NE)
        t_cb = tt(dve, v("cb"), v("cb"), v("n"), ALU.add, t_cb, t)
        t_le = tt(dve, le, small["cb"][0:1, 0:8].unsqueeze(1).to_broadcast([1, NBLK, NE]), numbers, ALU.is_le, t_cb)
        t_le = reduce(small["p2"][0:1, 0:NBLK], le, ALU.add, t_le, t_slot)
        t_eid = dve(lambda e: e.tensor_scalar(eid[:, :], small["p2"][0:1, 0:NBLK], float(NE - 1), None, ALU.min), t_le)

        t_scatter = []
        for b in range(NB):
            if b == 4:
                chunk_split(0, 4, 0)
                up_act(0, 3)
            if b:
                rows_normal(b)
            t = t_rowsx
            for k in range(2):
                ts = pool.load(lambda e, b=b, k=k: e.indirect_dma_start(
                    slots_d, bass.IndirectOffsetOnAxis(ap=slot[:, k, b:b + 1], axis=0), yb[b], None),
                    l_yg[b], t, t_slot, t_clear)
            t_scatter.append(ts)

        F_free = [done_b, None]
        E_free = [done_b, None]
        t_F, t_E = {}, {}
        PIECE = (0, 940, 1880, KC * 2 * NI, WE)

        def expert_load(j):
            def go(e):
                r = e.value_load(eid[0:1, j:j + 1], min_val=0, max_val=NE - 1)
                return e.dma_start(F[j % 2][:, :], wexp_d[bass.DynSlice(r, 1), :, :].rearrange("o p n -> (o p) n"))
            if j < NBLK:
                t_F[j] = sp.load(go, l_F[j % 2], t_eid, F_free[j % 2])
                t_E[j] = []

        def expert_split(j, p):
            if j >= NBLK:
                return
            i = j % 2
            z = slice(PIECE[p], PIECE[p + 1])
            t = copy_act(E[i][0][:, z], F[i][:, z], t_F[j], E_free[i])
            t_E[j].append(tt(pool if p % 2 else dve, E[i][1][:, z], F[i][:, z], E[i][0][:, z].bitcast(F32),
                             ALU.subtract, t))
            if p == 3:
                F_free[i] = list(t_E[j])

        xg_free = [done_b, done_b]
        xgT_free = done_b
        t_xg = {}
        t_xgT = None

        def rows_load(j):
            if j < NBLK:
                t_xg[j] = sp.load(lambda e: e.dma_start(
                    xg[j % 2][:, :, :], slots_d[j * BS:(j + 1) * BS, :].rearrange("(c p) d -> p c d", p=128)),
                    l_xg[j % 2], t_scatter, xg_free[j % 2])

        expert_load(0)
        up_pe(0, 4)
        chunk_split(0, 5, 0)
        down(0, 3)
        up_act(0, 4)
        expert_split(0, 0)
        expert_split(0, 1)
        up_pe(0, 5)
        down(0, 4)
        up_act(0, 5)
        expert_split(0, 2)
        expert_split(0, 3)
        up_pe(1, NS - 1, early=True)
        hx = over("hx", [128, HT], F32, place_t)
        (g, tg), (u, tu) = t_up.pop((1, NS - 1, 0)), t_up.pop((1, NS - 1, 1))
        s_ = sg[0][:, :]
        t = gu_free[g] = act(lambda e, g=g: e.activation(s_, GU[g][:, 0:HT], ACT.Silu), tg, sg_free[0])
        t_hx = gu_free[u] = sg_free[0] = tt(dve, hx[:, :], s_, GU[u][:, 0:HT], ALU.mult, t, tu, t_slot, t_eid, t_rank)
        rows_load(0)
        rows_load(1)
        F_free[1] = list(sf_free)
        expert_load(1)
        def turn_x(j, where=None):
            nonlocal t_xgT, xgT_free
            to_, free = where or (AC[2:4], [2, 3])
            fr = gu_free if where else ac_free
            if j >= NBLK:
                return
            t_h = []
            for c in range(2):
                for k in range(KC):
                    t = tr(to_[c][:, k * 128:(k + 1) * 128], xg[j % 2][:, c, k * 128:(k + 1) * 128], ident[:, :],
                           t_xg[j], fr[free[c]], inc=k == KC - 1)
                xg_free[j % 2] = t
                src = to_[c][:, :].rearrange("p (k t) -> p k t", k=KC)
                to = at(xgT, slice(None), slice(None), slice(c * 128, c * 128 + 128))
                fr[free[c]] = split(to, src, t, xgT_free)
                t_h.append(fr[free[c]])
            t_xgT = t_h

        yo_free = [t_scatter] * 4
        hT_free = [list(hs_free)]
        t_y = []
        hb_free = [list(sg_free) + list(hh_free) for _ in range(2)]

        def block(j):
            nonlocal xgT_free
            w = E[j % 2]
            t_hT = []
            expert_load(j + 2)
            for i, (o, n) in enumerate(IC):
                g = turn(n_gu, 4)
                for a in range(2):
                    for k in range(KC):
                        z = k * 2 * NI + a * NI + o
                        t = mm3(GU[g][0:n, a * BS:(a + 1) * BS], at(w, slice(None), slice(z, z + n)),
                                at(xgT, slice(None), k, slice(None)), k == 0, k == KC - 1, t_E[j][0:3], t_xgT, gu_free[g],
                                inc=k == KC - 1)
                q = i % 2
                s_, h_ = sg[q][0:n, 0:BS], hh[q][0:n, 0:BS]
                ta = act(lambda e, s_=s_, g=g, n=n: e.activation(s_, GU[g][0:n, 0:BS], ACT.Silu), t, hb_free[q])
                ta = gu_free[g] = tt(dve, h_, s_, GU[g][0:n, BS:2 * BS], ALU.mult, ta, hb_free[q])
                ta = split((hT[0][0:n, i, :], hT[1][0:n, i, :]), h_, ta, hT_free[0])
                hb_free[q] = ta
                t_hT.append(ta)
                if i < 2:
                    expert_split(j + 1, i)
                if j == NBLK - 1 and i == 0:
                    chunk_split(1, 0, 1024)
            if j == NBLK - 1:
                up_pe(1, 0)
                chunk_split(1, 1, 1024)
            xgT_free = t
            turn_x(j + 1)
            expert_split(j + 1, 2)
            for c, parts in ((0, (0, 1)), (1, (0, 1)), (0, (2,)), (1, (2,))):
                for i in parts:
                    n = IC[i][1]
                    z = KC * 2 * NI + i * D
                    t = mm3(AC[c][:, :], (hT[0][0:n, i, c * 128:c * 128 + 128], hT[1][0:n, i, c * 128:c * 128 + 128]),
                            (w[0][0:n, z:z + D], w[1][0:n, z:z + D]), i == 0, i == 2, t_E[j], t_hT[i], ac_free[c], inc=i == 2)
                if parts[-1] < 2:
                    continue
                y = (2 * j + c) % 4
                ac_free[c] = copy_act(yg[y][:, :], AC[c][:, :], t, yo_free[y])
                yo_free[y] = sp.load(lambda e, y=y, c=c: e.dma_start(
                    y_d[j * BS + c * 128:j * BS + c * 128 + 128, :], yg[y][:, :]), l_yo[y], ac_free[c])
            expert_split(j + 1, 3)
            rows_load(j + 2)
            hT_free[0] = t
            E_free[j % 2] = t

        g = turn(n_gu, 4), turn(n_gu, 4)
        turn_x(0, ([GU[i] for i in g], g))
        down(0, 5)
        E_free[1] = list(slot_free) + list(hs_free)
        sg[1], hh[1], hs[1] = sg1, hh1, hs1
        t_xs = [None] * NB
        for b in range(4):
            ac_free[b] = t_xs[b] = tt(dve, xs[:, b, :], xs[:, b, :], AC[b][0:T, :], ALU.add, t_ac[b], t_rowsx)
        for j in range(NBLK):
            if j == NBLK - 2:
                assert j % 2 == 0
                sf_free[:] = [list(F_free[0])] * 2
                chunk_load(1, 0)
                chunk_load(1, 1)
            if j == NBLK - 1:
                slot_free[1:3] = [E_free[0]] * 2
            block(j)

        t_wrote = list(yo_free)
        yb_free = list(yo_free) + [xg_free[0]] * 2 + [xg_free[1]] * 2
        hs_free[:] = [hT_free[0]] * 2
        sg_free[:], hh_free[:] = hb_free, hb_free
        back = [(b, k) for b in (4, 5, 6, 7, 0, 1, 2, 3) for k in range(2)]
        t_back = {}

        def gather(n):
            b, k = back[n]
            i = n % 8
            t_back[n] = pool.load(lambda e: e.indirect_dma_start(
                yb[i], None, y_d, bass.IndirectOffsetOnAxis(ap=slot[:, k, b:b + 1], axis=0)),
                l_yg[i], t_wrote, yb_free[i])

        t_end = []

        def add_back(n):
            b, k = back[n]
            i = n % 8
            yb_free[i] = t_xs[b] = dve(lambda e: e.scalar_tensor_tensor(
                xs[:, b, :], yb[i], w01[:, k, b:b + 1], xs[:, b, :], ALU.mult, ALU.add),
                t_back[n], t_xs[b], t_w01, t_rowsx)
            if k and b < 4:
                t_end.append(sp.load(lambda e: e.dma_start(out_d[b], xs[:, b, :]), l_out, t_xs[b]))

        chunk_load(1, 2)
        for n in range(8):
            gather(n)
        up_act(1, 0)
        chunk_split(1, 2, 0)
        hx2 = [over(f"hx{n}", [128, HT], F32R, EW[1] + i * HT * 4) for i, n in enumerate(("hi", "lo"))]
        t_hs[1, NS - 1] = split(at(hx2, slice(None), slice(None)), hx[:, :], t_hx, E_free[1])
        for c in range(1, NS - 1):
            up_pe(1, c)
            down(1, c - 1)
            up_act(1, c)
            if c + 2 < NS:
                o = 1024 if c + 2 == NS - 1 else 0
                chunk_load(1, c + 2, o)
                chunk_split(1, c + 2, 0, o)
            for n in range(4 * (c - 1), 4 * c):
                add_back(n)
                if n + 8 < 16:
                    gather(n + 8)
        down(1, NS - 1, h=hx2)
        down(1, NS - 2)
        for b in range(4, NB):
            t = tt(dve, xs[:, b, :], xs[:, b, :], AC[b - 4][0:T, :], ALU.add, t_ac[b], t_xs[b])
            t_end.append(sp.load(lambda e, b=b: e.dma_start(out_d[b], xs[:, b, :]), l_out, t))
        sp.needs(t_end[-1])

        with nc.Block() as block:
            block.sync(sp.play)
            block.gpsimd(pool.play)
            block.scalar(act.play)
            block.vector(dve.play)
            block.tensor(pe.play)


def kernel(x, ctx_2048, L0_attn_W_K, L0_attn_W_Q, L0_attn_W_V, L0_attn_W_O, L0_xattn_Wq, L0_xattn_Wk, L0_xattn_Wv,
           L0_ffn_gate_w, L0_ffn_expert_gate, L0_ffn_expert_up, L0_ffn_expert_down, L0_ffn_shared_gate,
           L0_ffn_shared_up, L0_ffn_shared_down):
    import numpy as np
    import concourse.bacc as bacc
    from concourse.bass_utils import run_bass_kernel_spmd

    def c(a):
        return np.ascontiguousarray(a)

    def inner(a):
        a = np.asarray(a)
        a = np.swapaxes(a, -1, -2)
        a = a.reshape(a.shape[:-2] + (KC, 128, a.shape[-1]))
        return np.swapaxes(a, -2, -3)

    wk, wq, wv = (np.asarray(a) for a in (L0_attn_W_K, L0_attn_W_Q, L0_attn_W_V))
    wqk = inner(np.concatenate([wq, wk], axis=1))
    wvp = inner(wv.reshape(NH // 2, 2 * DH, D))
    wo = np.asarray(L0_attn_W_O).T.reshape(NH // 2, 2, DH, D).transpose(0, 2, 1, 3)
    ctx = inner(np.asarray(ctx_2048).reshape(NB, MC, MS, D))
    wcat = np.concatenate([np.asarray(L0_xattn_Wk), np.asarray(L0_xattn_Wv)], axis=0)
    wcat = wcat.reshape(2, XH, 16, 2, D).transpose(0, 3, 1, 2, 4).reshape(2 * 512, D)
    wkv = inner(wcat).reshape(128, KC * 1024)
    wqx = inner(L0_xattn_Wq).reshape(128, KC * D)
    gw = inner(L0_ffn_gate_w)
    up = np.zeros((2, NS * 128, D), np.float32)
    up[0, :2 * NI] = np.asarray(L0_ffn_shared_gate)
    up[1, :2 * NI] = np.asarray(L0_ffn_shared_up)
    dn = np.zeros((NS * 128, D), np.float32)
    dn[:2 * NI] = np.asarray(L0_ffn_shared_down).T
    upc = inner(up.reshape(2, NS, 128, D).transpose(1, 0, 2, 3).reshape(NS, 256, D)).reshape(NS, 128, KC * 256)
    moe = np.concatenate([upc, dn.reshape(NS, 128, D)], axis=2)
    eup = inner(np.concatenate([np.asarray(L0_ffn_expert_gate), np.asarray(L0_ffn_expert_up)], axis=1))
    edn = np.zeros((NE, 3 * 128, D), np.float32)
    edn[:, :NI] = np.asarray(L0_ffn_expert_down).transpose(0, 2, 1)
    edn = edn.reshape(NE, 3, 128, D).transpose(0, 2, 1, 3).reshape(NE, 128, 3 * D)
    wexp = np.concatenate([eup.reshape(NE, 128, KC * 2 * NI), edn], axis=2)
    e = np.arange(NE)
    row = np.concatenate([(e[None, :] < e[:, None]).reshape(-1), np.repeat(np.arange(NBLK), NE)])
    cst = np.concatenate([np.triu(np.ones((T, T)), 1), np.tile(row, (T, 1))], axis=1).astype(np.float32)
    i = np.arange(T)
    arrays = {
        "x": c(x).reshape(7, 128, D), "ctx": c(ctx), "wqk": c(wqk), "wv": c(wvp), "wo": c(wo), "wqx": c(wqx), "wkv": c(wkv), "gw": c(gw),
        "moe": c(moe), "wexp": c(wexp), "ident": np.eye(128, dtype=np.float32),
        "mask": np.where(i[:, None] >= i[None, :], 0.0, -1e10).astype(np.float32),
        "cst": c(cst),
    }
    nc = bacc.Bacc("TRN2", target_bir_lowering=False, num_devices=1)
    args = [nc.dram_tensor(k, a.shape, mybir.dt.from_np(a.dtype), kind="ExternalInput").ap() for k, a in arrays.items()]
    out = nc.dram_tensor("out", (NB, T, D), F32, kind="ExternalOutput").ap()
    decoder_layer(nc, *args, out)
    r = run_bass_kernel_spmd(nc, [arrays], core_ids=[0])
    return r.results[0]["out"]
```
